# Optimizing a Trainium2 kernel written in Bass

```python
import numpy as np
import jax
import jax.numpy as jnp

def _softmax(x, axis=-1):
    return jax.nn.softmax(x, axis=axis)

def _gelu(x):
    return jax.nn.gelu(x, approximate=True)

def _silu(x):
    return jax.nn.silu(x)

def _sigmoid(x):
    return jax.nn.sigmoid(x)

def _layernorm(x, axis=-1, eps=1e-05):
    m = jnp.mean(x, axis=axis, keepdims=True)
    v = jnp.var(x, axis=axis, keepdims=True)
    return (x - m) / jnp.sqrt(v + eps)

def _scatter_add(tgt, idx, src, axis=0):
    return tgt.at[idx].add(src)

def _segment_sum(src, seg, n):
    return jax.ops.segment_sum(src, seg, n)
kernel_name = 'mk_xattn_ffn_d1_seqx_r4_6f6e0c'

def setup_inputs(seed: int=0):
    np.random.seed(seed)
    _w = jnp.asarray

    def _rec_inputs():
        import jax
        import jax.numpy as jnp
        _rk = jax.random.key(seed)
        x = 7.22e-05 + 1 * jax.random.normal(jax.random.fold_in(_rk, 1), (8, 512, 512), jnp.float32)
        _lenS = 512 - jax.random.randint(jax.random.fold_in(_rk, 7), (8,), 0, max(1, 512 // 4) + 1, jnp.int32)
        _lenS2 = 1601 - jax.random.randint(jax.random.fold_in(_rk, 8), (8,), 0, max(1, 1601 // 4) + 1, jnp.int32)
        _ctx_512P = jax.random.normal(jax.random.fold_in(_rk, 11), (8, 16, 128), jnp.float32)
        _ctx_512c = jax.random.dirichlet(jax.random.fold_in(_rk, 511), 0.3 * jnp.ones((16,), jnp.float32), (8, 1601))
        _ctx_512t = jnp.einsum('bsk,bkd->bsd', _ctx_512c, _ctx_512P)
        _ctx_512t = _ctx_512t * jax.lax.rsqrt(jnp.mean(jnp.square(_ctx_512t)) + 1e-12) * 0.953939
        ctx_512 = -0.000514642 + 1.00011 * (_ctx_512t + 0.3 * jax.random.normal(jax.random.fold_in(_rk, 611), (8, 1601, 128), jnp.float32))
        return (x, ctx_512)
    x, ctx_512 = _rec_inputs()

    def _L0_xattn_setup():
        import jax, jax.numpy as jnp
        import numpy as np
        B, S, H, NH, L = (2, 512, 512, 16, 128)
        HD = H // NH
        key = jax.random.key(seed)
        k1, k2, k3, k4, k5 = jax.random.split(key, 5)
        scale = 0.02
        return {'q': jax.random.normal(k1, (B, S, H), dtype=jnp.float32), 'latent_kv': jax.random.normal(k2, (B, S, L), dtype=jnp.float32), 'Wq': jax.random.normal(k3, (H, H), dtype=jnp.float32) * scale, 'Wkv_expand': jax.random.normal(k4, (2 * H, L), dtype=jnp.float32) * scale, 'Wout': jax.random.normal(k5, (H, H), dtype=jnp.float32) * scale}
    _L0_xattn_all = _L0_xattn_setup()
    _L0_xattn_in = {k: v for k, v in _L0_xattn_all.items() if k in ('Wq', 'Wkv_expand', 'Wout')}
    del _L0_xattn_all

    def _L0_ffn_setup():
        import jax, jax.numpy as jnp
        import numpy as np
        TOP_K = 2
        key = jax.random.key(seed)
        k1, k2, k3, k4, k5 = jax.random.split(key, 5)
        B, S, H, O, E = (2, 256, 512, 512, 8)
        hidden_states = jax.random.normal(k1, (B, S, H), dtype=jnp.float32)
        router_w = jax.random.normal(k2, (O * E, H), dtype=jnp.float32) * 0.02
        router_b = jnp.zeros((O * E,), dtype=jnp.float32)
        expert_w = jax.random.normal(k3, (E, O, H), dtype=jnp.float32) * 0.02
        expert_b = jnp.zeros((E, O), dtype=jnp.float32)
        return {'hidden_states': hidden_states, 'router_w': router_w, 'router_b': router_b, 'expert_w': expert_w, 'expert_b': expert_b}
    _L0_ffn_all = _L0_ffn_setup()
    _L0_ffn_in = {k: v for k, v in _L0_ffn_all.items() if k in ('router_w', 'router_b', 'expert_w', 'expert_b')}
    del _L0_ffn_all
    return {'x': x, 'ctx_512': ctx_512, 'L0_xattn_Wq': _L0_xattn_in['Wq'], 'L0_xattn_Wkv_expand': _L0_xattn_in['Wkv_expand'], 'L0_xattn_Wout': _L0_xattn_in['Wout'], 'L0_ffn_router_w': _L0_ffn_in['router_w'], 'L0_ffn_router_b': _L0_ffn_in['router_b'], 'L0_ffn_expert_w': _L0_ffn_in['expert_w'], 'L0_ffn_expert_b': _L0_ffn_in['expert_b']}

def reference(x, ctx_512, L0_xattn_Wq, L0_xattn_Wkv_expand, L0_xattn_Wout, L0_ffn_router_w, L0_ffn_router_b, L0_ffn_expert_w, L0_ffn_expert_b):
    import jax
    import jax.numpy as jnp

    def _L0_xattn_ref(q, latent_kv, Wq, Wkv_expand, Wout):
        import jax, jax.numpy as jnp
        import numpy as np
        B, S, H, NH, L = (2, 512, 512, 16, 128)
        HD = H // NH
        b, sq, _ = q.shape
        sk = latent_kv.shape[1]
        qp = q @ Wq.T
        kv = latent_kv @ Wkv_expand.T
        k, v = jnp.split(kv, 2, axis=-1)
        qh = qp.reshape(b, sq, NH, HD).transpose(0, 2, 1, 3)
        kh = k.reshape(b, sk, NH, HD).transpose(0, 2, 1, 3)
        vh = v.reshape(b, sk, NH, HD).transpose(0, 2, 1, 3)
        inv_sqrt_d = 1.0 / jnp.sqrt(jnp.float32(HD))
        scores = jnp.einsum('bhqd,bhkd->bhqk', qh, kh) * inv_sqrt_d
        causal = jnp.tril(jnp.ones((sq, sk), dtype=bool))
        scores = jnp.where(causal, scores, jnp.finfo(scores.dtype).min)
        attn = jax.nn.softmax(scores, axis=-1)
        out = jnp.einsum('bhqk,bhkd->bhqd', attn, vh)
        out = out.transpose(0, 2, 1, 3).reshape(b, sq, H)
        return out @ Wout.T

    def _L0_ffn_ref(hidden_states, router_w, router_b, expert_w, expert_b):
        import jax, jax.numpy as jnp
        import numpy as np
        TOP_K = 2
        B, S, H = hidden_states.shape
        E, O, _ = expert_w.shape
        T = B * S
        h = hidden_states.reshape(T, H)
        logits = (h @ router_w.T + router_b).reshape(T, O, E)
        probs = jax.nn.softmax(logits.astype(jnp.float32), axis=-1)
        w, sel = jax.lax.top_k(probs, TOP_K)
        w = w / jnp.sum(w, axis=-1, keepdims=True)
        w = w.astype(h.dtype)
        t_idx = jnp.arange(T)[:, None, None]
        c = jnp.zeros((T, E), dtype=h.dtype).at[t_idx, sel].add(w)
        expert_out = jnp.einsum('th,eoh->teo', h, expert_w) + expert_b[None, :, :]
        final = jnp.einsum('te,teo->to', c, expert_out)
        return final.reshape(B, S, O)
    x = x + _L0_xattn_ref(_layernorm(x, axis=-1), ctx_512, L0_xattn_Wq, L0_xattn_Wkv_expand, L0_xattn_Wout)
    x = x + _L0_ffn_ref(_layernorm(x, axis=-1), L0_ffn_router_w, L0_ffn_router_b, L0_ffn_expert_w, L0_ffn_expert_b)
    return x

_drawn_inputs = setup_inputs


def setup_inputs(seed=0):
    import zlib

    import numpy as np

    out = dict(_drawn_inputs(seed))
    spreads = {'L0_ffn_router_b': (0.0, 0.1), 'L0_ffn_expert_b': (0.0, 0.1)}
    factors = {'L0_xattn_Wq': 22.881}
    for name, (base, spread) in spreads.items():
        noise = np.random.default_rng([zlib.crc32(name.encode()), seed]).standard_normal(out[name].shape)
        drawn = base * np.exp(spread * noise) if base else spread * noise
        out[name] = jnp.asarray(drawn.astype(out[name].dtype))
    for name, factor in factors.items():
        out[name] = (out[name] * factor).astype(out[name].dtype)
    return out
```

```python
from contextlib import ExitStack

import concourse.bass as bass
from concourse import mybir

ALU = mybir.AluOpType
ACT = mybir.ActivationFunctionType
F32 = mybir.dt.float32
F32R = mybir.dt.float32r
BF16 = mybir.dt.bfloat16
AX_X = mybir.AxisListType.X

P = 128
B, S, H = 8, 512, 512
NH, HD = 16, 32
KC = H // P
QB = S // P
HC = P // HD
NE, O = 8, 512
NT = B * S // P
NB = B * KC
UNITS = QB * 2
LAG = 2
STACK = 3 * HD
STACK_DMAS = 3 * HC
SCALE = float(HD) ** -0.5
EPS = 1e-5
MASKED = -1e30
BIAS_PARTS = 3


def build(nc, x, ctxT, wqT, wkvT, woT, routerT, router_b, expertT, expert_b, out):
    ctx = ExitStack()
    with ctx:
        def sem(name):
            return ctx.enter_context(nc.semaphore(name))

        size = {F32: 4, F32R: 4, BF16: 2}
        start = (nc.sbuf_base + 63) // 64 * 64

        class Place:

            def __init__(self, at):
                self.at = at

            def __call__(self, name, shape, dtype, at=None):
                n = size[dtype]
                for d in shape[1:]:
                    n *= d
                if at is None:
                    at = self.at
                    self.at += (n + 31) // 32 * 32
                assert at + n <= nc.sbuf_usable_end, (name, at + n)
                return nc.alloc_sbuf_tensor_at(name, shape, dtype, offset=at)

        keep = Place(start)
        ident = keep("ident", [P, P], F32)
        identb = keep("identb", [P, P], BF16)
        maskb = keep("maskb", [P, P], BF16)
        c_all = keep("c_all", [P, NT, NE], F32)
        stats = keep("stats", [P, 2, 6], F32)
        moments = keep("moments", [P, 2, 2], F32)
        rstd = keep("rstd", [P, 2], F32)
        minus_one = keep("minus_one", [P, 1], F32)
        minus_half = keep("minus_half", [P, 1], F32)
        eps = keep("eps", [P, 1], F32)
        zero = keep("zero", [P, 1], F32)
        turn = keep("turn", [P, 1], F32)

        att = Place(keep.at)
        wq_h = att("wq_h", [P, KC, H], F32R)
        wq_l = att("wq_l", [P, KC, H], F32R)
        wkv_h = att("wkv_h", [P, 2 * H], F32R)
        wkv_l = att("wkv_l", [P, 2 * H], F32R)
        wo_h = att("wo_h", [P, KC, H], F32R)
        wo_l = att("wo_l", [P, KC, H], F32R)
        xt = att("xt", [P, QB, H], F32)
        xr = att("xr", [P, QB, H], F32)
        xn = att("xn", [P, 2, H], F32)
        xnT_h = att("xnT_h", [P, KC, S], F32R)
        xnT_l = att("xnT_l", [P, KC, S], F32R)
        ctx_raw = att("ctx_raw", [P, S], F32)
        ctx_h = att("ctx_h", [P, S], F32R)
        ctx_l = att("ctx_l", [P, S], F32R)
        v_sb = att("v_sb", [P, QB, H], F32)
        qk = att("qk", [P, 4, S], F32R)
        QH, QL, KH, KL = range(4)
        qk_st = [att(f"qk_st{i}", [P, HC, 2, S], F32R) for i in range(2)]
        probs = att("probs", [P, 4, 2, S], F32)
        pT_at = att.at
        pT = att("pT", [P, HC, QB, S], F32)
        r_sb = att("r_sb", [P, S], F32)
        r_rep = att("r_rep", [P, QB, HC, HD], F32)
        recip = att("recip", [P, QB, HC], F32)
        sums = att("sums", [P, 2, QB, HC], F32)
        rmax = att("rmax", [P, 4, 2], F32)
        nmax = att("nmax", [P, 4, 2], F32)
        o_sb = att("o_sb", [P, S], F32)
        oT_h = att("oT_h", [P, KC, S], F32R)
        oT_l = att("oT_l", [P, KC, S], F32R)
        raw = Place(pT_at)
        wq_raw = raw("wq_raw", [P, KC, H], F32)
        wkv_raw = raw("wkv_raw", [P, 2 * H], F32)
        wo_raw = raw("wo_raw", [P, KC, H], F32)

        ffn = Place(keep.at)
        raw_at = ffn.at
        w_l = ffn("w_l", [P, NE, KC, O], F32R)
        w_raw = ffn("w_raw", [P, NE, KC, O], F32, at=raw_at)
        w_h = ffn("w_h", [P, NE, KC, O], F32R)
        xb = [ffn(f"xb{i}", [P, H], F32) for i in range(2)]
        hT_h = [ffn(f"hT_h{i}", [P, KC, P], F32R) for i in range(2)]
        hT_l = [ffn(f"hT_l{i}", [P, KC, P], F32R) for i in range(2)]
        bias_sel = ffn("bias_sel", [P, NE, P], BF16)
        bias_rows = ffn("bias_rows", [P, O], BF16)
        logits_at = ffn.at
        logits = [ffn(f"logits{i}", [P, NE, O], F32) for i in range(2)]
        top_at = ffn.at
        top_a = ffn("top_a", [P, 4, O], F32)
        top_b = ffn("top_b", [P, 4, O], F32)
        second = ffn("second", [P, O], F32)
        gap = ffn("gap", [P, O], F32)
        th = ffn("th", [P, O], F32)
        w2 = ffn("w2", [P, O], F32)
        top_c = ffn("top_c", [P, 2, O], F32, at=ffn.at)
        taken = ffn("taken", [P, 3, O], BF16)
        scrap = ffn("scrap", [P, 2, O], BF16)
        tanh_sum = ffn("tanh_sum", [P, 2, NE], F32)
        th_sum = ffn("th_sum", [P, 2], F32)
        sign_sum = ffn("sign_sum", [P, 2, NE], F32)
        c_first = ffn("c_first", [P, NE], F32)
        c_taken = ffn("c_taken", [P, 2, NE + 1], F32)
        c_diff = ffn("c_diff", [P, NE], F32)
        bias_raw = ffn("bias_raw", [P, O], F32, at=top_at)
        bias_rest = ffn("bias_rest", [P, O], F32, at=top_at + 4 * O)
        exp_ = Place(logits_at)
        hn = exp_("hn", [P, H], F32)
        eb = exp_("eb", [P, O], F32)
        c_pad = [exp_(f"c_pad{i}", [P, P], F32) for i in range(2)]
        cT = [exp_(f"cT{i}", [P, P], F32) for i in range(2)]

        x1 = nc.dram_tensor("x1", [NT * P, H], F32, kind="Internal").ap()

        ps = [ctx.enter_context(nc.psum_tensor(f"ps{i}", [P, 512], F32)) for i in range(8)]
        s_ps = ps[0:4]
        t_ps = ps[4:6]
        o_ps = ps[6]
        j_ps = ps[7]
        l_ps = ps[0:4]
        over = ps[4:6]
        junk = ps[6]
        h_ps = ps[7]
        c_ps = ps[6]
        b_ps = ps[5]

        names = """
            const_z const_one const_mask w_in w_hi w_lo x_in ctx_in ln_st ln_var ln_rs xn_ok xT_mm xT_hi xT_lo ctx_split q_mm q_hi q_lo
            k_mm k_hi k_lo stacked v_mm v_ok scores rowmax negmax exps turned pt_act pt_dve pv recips
            reps r_mm r_ok o_ok o_hi o_lo wo_mm x1_ok xr_in x1_out
            fw_hi fw_lo bias_in bias_zero bias_split bias_rest_ok bias_put sel_z sel_ok xb_in ln2_st ln2_var ln2_rs hn_ok
            hT_mm hT_hi hT_lo lg_mm lg_ok top gap_ok th_ok second_ok u_ok w2_ok count first_step c_sum c_half c_ok
            ew_hi ew_lo eb_in xe_in ln3_st ln3_var ln3_rs en_ok eT_mm eT_hi eT_lo pad_z c_put cT_mm cT_ok cb_mm
            y_mm acc y_out
        """.split()
        names += [f"raw{e}_in" for e in range(NE)]
        s = {n: sem(n) for n in names}

        def some(value):
            return not isinstance(value, int) or value > 0

        COUNTS = NE
        FIRSTS = NE * 3

        def f32(ap):
            return ap.bitcast(F32)

        def three(pe, dst, lh, ll, rh, rl, start, stop):
            pe.matmul(dst, lh, rh, start=start, stop=False)
            pe.matmul(dst, lh, rl, start=False, stop=False)
            return pe.matmul(dst, ll, rh, start=False, stop=stop)

        def before(c, v):
            k = c * UNITS + v - LAG
            return (k // (KC * UNITS), k % (KC * UNITS) // UNITS, k % UNITS)

        def fillers(c, v, first, last):
            found = []
            if v == 0 and not (last and c == KC - 1):
                found.append(("K", None))
            if v == 1 and not (last and c == KC - 1):
                found.append(("Q", None))
            if v == 2 and not (first and c == 0):
                found.append(("R", None))
            if c == 0 and v >= 4:
                found.append(("V", v - 4))
            if c == 1 and v >= 4 and not first:
                found.append(("WO", v - 4))
            if c == 2 and v >= 4 and not last:
                found.append(("LNT", v - 4))
            return found

        def over_batches(eng, body, epilogue):
            body(0, True, False)
            with eng.Fori(1, B - 1) as b:
                body(b, False, False)
            body(B - 1, False, True)
            epilogue()

        block = ctx.enter_context(nc.Block())

        @block.sync
        def _(sp):
            sp.dma_start(wq_raw[:], wqT.rearrange("(c p) n -> p c n", p=P)).then_inc(s["w_in"], 16)
            sp.dma_start(wkv_raw[:], wkvT).then_inc(s["w_in"], 16)
            sp.dma_start(wo_raw[:], woT.rearrange("(c p) n -> p c n", p=P)).then_inc(s["w_in"], 16)
            sp.dma_start(xt[:], x[0:S, :].rearrange("(i p) h -> p i h", p=P)).then_inc(s["x_in"], 16)
            sp.dma_start(ctx_raw[:], ctxT[0:P, :]).then_inc(s["ctx_in"], 16)

            def stack(n, par, stored=0):
                sp.wait_ge(s["k_hi"], n + 1)
                sp.wait_ge(s["k_lo"], n + 1)
                sp.wait_ge(s["q_hi"], n + 1)
                sp.wait_ge(s["q_lo"], n + 1)
                for g, (q, k) in enumerate(((QH, KH), (QL, KH), (QH, KL))):
                    if g == 2 and some(stored):
                        sp.wait_ge(s["x1_out"], stored)
                    for hh in range(HC):
                        sp.dma_start(f32(qk_st[par][g * HD:(g + 1) * HD, hh]),
                                     f32(qk[hh * HD:(hh + 1) * HD, q:k + 1:k - q])).then_inc(s["stacked"], 16)

            def tokens(ap, b):
                return ap[bass.ds(b * S, S), :].rearrange("(i p) h -> p i h", p=P)

            def body(b, first, last):
                for c in range(KC):
                    n = b * KC + c
                    if c == 0 and not first:
                        sp.dma_start(xr[:], tokens(x, b - 1)).then_inc(s["xr_in"], 16)
                    if c == 1 and not last:
                        sp.wait_ge(s["xn_ok"], (b + 1) * QB)
                        sp.dma_start(xt[:], tokens(x, b + 1)).then_inc(s["x_in"], 16)
                        sp.wait_ge(s["ctx_split"], (b + 1) * 2)
                        sp.dma_start(ctx_raw[:], ctxT[bass.ds((b + 1) * P, P), :]).then_inc(s["ctx_in"], 16)
                    if not (last and c == KC - 1):
                        stack(n + 1, (c + 1) % 2, 0 if first or c < KC - 1 else b * 16)
                    if c == 1 and not first:
                        sp.wait_ge(s["x1_ok"], b * QB)
                        sp.dma_start(tokens(x1, b - 1), xr[:]).then_inc(s["x1_out"], 16)

            def epilogue():
                sp.wait_ge(s["x1_out"], (B - 1) * 16)
                sp.dma_start(xr[:], tokens(x, B - 1)).then_inc(s["xr_in"], 16)
                sp.wait_ge(s["x1_ok"], B * QB)
                sp.dma_start(tokens(x1, B - 1), xr[:]).then_inc(s["x1_out"], 16)
                sp.wait_ge(s["x1_out"], B * 16)

            stack(0, 0)
            over_batches(sp, body, epilogue)

            r_v = routerT.rearrange("(c p) e o -> p e c o", p=P)
            e_v = expertT.rearrange("(c p) e o -> p e c o", p=P)

            def load_block(t, i, name):
                if some(t * 16):
                    sp.wait_ge(s[name], t * 16)
                sp.dma_start(xb[i][:], x1[bass.ds(t * P, P), :]).then_inc(s[name], 16)

            load_block(0, 0, "xb_in")
            sp.wait_ge(s["bias_zero"], 1)
            sp.dma_start(bias_raw[0:NE, :], router_b).then_inc(s["bias_in"], 16)
            for e in range(NE):
                sp.dma_start(w_raw[:, e], r_v[:, e]).then_inc(s[f"raw{e}_in"], 16)
            load_block(1, 1, "xb_in")
            for k in range(BIAS_PARTS):
                sp.wait_ge(s["bias_split"], k + 1)
                sp.dma_start(bias_rows[k * NE:(k + 1) * NE, :], taken[0:NE, k, :]).then_inc(s["bias_put"], 16)

            def router_pair(t, more):
                for i in range(2):
                    if more:
                        sp.wait_ge(s["hT_mm"], t + i + 1)
                        load_block(t + i + 2, i, "xb_in")

            with sp.Fori(0, NT // 2 - 1) as pair:
                t = pair * 2
                router_pair(t, True)
            sp.wait_ge(s["hT_mm"], NT - 1)
            load_block(0, 0, "xe_in")
            sp.wait_ge(s["hT_mm"], NT)
            load_block(1, 1, "xe_in")
            for e in range(NE):
                sp.wait_ge(s["lg_mm"], (NT - 1) * NE + e + 1)
                sp.dma_start(w_raw[:, e], e_v[:, e]).then_inc(s[f"raw{e}_in"], 16)
            sp.wait_ge(s["pad_z"], 1)
            sp.dma_start(eb[0:NE, :], expert_b).then_inc(s["eb_in"], 16)

            def expert_pair(t, more):
                for i in range(2):
                    sp.wait_ge(s["acc"], (t + i + 1) * (NE + 1))
                    sp.dma_start(out[bass.ds((t + i) * P, P), :], xb[i][:]).then_inc(s["y_out"], 16)
                    if more:
                        sp.wait_ge(s["y_out"], (t + i + 1) * 16)
                        load_block(t + i + 2, i, "xe_in")

            with sp.Fori(0, NT // 2 - 1) as pair:
                t = pair * 2
                expert_pair(t, True)
            expert_pair(NT - 2, False)
            sp.wait_ge(s["y_out"], NT * 16)

        @block.tensor
        def _(pe):
            def freed(task, k):
                for name in {"Q": ("q_hi", "q_lo"), "K": ("k_hi", "k_lo"), "V": ("v_ok",), "R": ("r_ok",),
                             "LNT": ("xT_hi", "xT_lo"), "WO": ("x1_ok",)}[task]:
                    pe.wait_ge(s[name], k + 1)

            def norm_turn(g, i):
                pe.wait_ge(s["xn_ok"], g + 1)
                for k in range(KC):
                    mm = pe.transpose(j_ps[:, k * P:(k + 1) * P], xn[:, i % 2, k * P:(k + 1) * P], ident[:])
                mm.then_inc(s["xT_mm"], 1)

            def queries(n, c):
                if c == 0:
                    pe.wait_ge(s["xT_hi"], n + QB)
                    pe.wait_ge(s["xT_lo"], n + QB)
                cols = slice(c * P, (c + 1) * P)
                for k in range(KC):
                    mm = three(pe, j_ps[:], wq_h[:, k, cols], wq_l[:, k, cols], xnT_h[:, k, :], xnT_l[:, k, :],
                               k == 0, k == KC - 1)
                mm.then_inc(s["q_mm"], 1)

            def keys(c, b):
                if c == 0:
                    pe.wait_ge(s["ctx_split"], (b + 1) * 2)
                cols = slice(c * P, (c + 1) * P)
                three(pe, j_ps[:], wkv_h[:, cols], wkv_l[:, cols], ctx_h[:], ctx_l[:], True, True)\
                    .then_inc(s["k_mm"], 1)

            def values(kb):
                rows = slice(kb * P, (kb + 1) * P)
                three(pe, j_ps[:], ctx_h[:, rows], ctx_l[:, rows], wkv_h[:, H:2 * H], wkv_l[:, H:2 * H], True, True)\
                    .then_inc(s["v_mm"], 1)

            def turn_recips(n):
                pe.wait_ge(s["reps"], n + 1)
                for i in range(QB):
                    mm = pe.transpose(j_ps[:, i * P:(i + 1) * P], r_rep[:, i].rearrange("p a d -> p (a d)"), ident[:])
                mm.then_inc(s["r_mm"], 1)

            def project_out(b, i):
                pe.wait_ge(s["o_hi"], (b + 1) * KC)
                pe.wait_ge(s["o_lo"], (b + 1) * KC)
                rows = slice(i * P, (i + 1) * P)
                for c in range(KC):
                    mm = three(pe, j_ps[:], oT_h[:, c, rows], oT_l[:, c, rows], wo_h[:, c, :], wo_l[:, c, :],
                               c == 0, c == KC - 1)
                mm.then_inc(s["wo_mm"], 1)

            def turn_probs(u, k, v):
                pe.wait_ge(s["exps"], u + 1)
                i = v // 2
                for j in range(2):
                    if some(u):
                        pe.wait_ge(s[("pt_act", "pt_dve")[j]], u)
                    for kb in range(i + 1):
                        mm = pe.transpose(t_ps[j][:, kb * P:(kb + 1) * P], probs[:, k, j, kb * P:(kb + 1) * P], ident[:])
                    mm.then_inc(s["turned"], 1)

            def values_of(n, c, b):
                pe.wait_ge(s["pt_act"], (n + 1) * UNITS)
                pe.wait_ge(s["pt_dve"], (n + 1) * UNITS)
                pe.wait_ge(s["v_ok"], (b + 1) * QB)
                if some(n):
                    pe.wait_ge(s["o_ok"], n)
                for kb in range(QB):
                    for hh in range(HC):
                        h = c * HC + hh
                        mm = pe.matmul(o_ps[hh * HD:(hh + 1) * HD, kb * P:S], v_sb[:, kb, h * HD:(h + 1) * HD],
                                       pT[:, hh, kb, kb * P:S], start=(kb == 0), stop=(kb == QB - 1),
                                       tile_position=(0, hh * HD), skip_group_check=True)
                mm.then_inc(s["pv"], 1)

            pe.wait_ge(s["const_one"], 2)
            pe.wait_ge(s["w_hi"], 3)
            pe.wait_ge(s["w_lo"], 3)
            for i in range(QB):
                if i:
                    freed("LNT", i - 1)
                norm_turn(i, i)
            freed("LNT", QB - 1)
            keys(0, 0)
            freed("K", 0)
            queries(0, 0)
            pe.wait_ge(s["const_mask"], 1)

            def body(b, first, last):
                prev = ("Q", 0) if first else ("R", b * KC - 2)
                for c in range(KC):
                    n = b * KC + c
                    for v in range(UNITS):
                        u = n * UNITS + v
                        i, slot = v // 2, v % 2
                        w = (i + 1) * P
                        if v == 0:
                            pe.wait_ge(s["stacked"], (n + 1) * (16 * STACK_DMAS))
                        if some(u - 1):
                            pe.wait_ge(s["exps"], u - 1)
                        for j in range(2):
                            hh = 2 * (v % 2) + j
                            bank = s_ps[2 * slot + j]
                            pe.matmul(bank[:, 0:w], qk_st[c % 2][0:STACK, hh, 0, i * P:w], qk_st[c % 2][0:STACK, hh, 1, 0:w],
                                      start=True, stop=False)
                            mm = pe.matmul(bank[:, i * P:w], identb[:], maskb[:], start=False, stop=True)
                        mm.then_inc(s["scores"], 1)
                        if v == LAG and not (first and c == 0):
                            values_of(n - 1, (c - 1) % KC, b if c else b - 1)
                        db, _, vv = before(c, v)
                        if not (first and db < 0):
                            turn_probs(u - LAG, (v - LAG) % 4, vv)
                        for task, k in fillers(c, v, first, last):
                            freed(*prev)
                            if task == "Q":
                                queries(n + 1, (c + 1) % KC)
                                prev = (task, n + 1)
                            elif task == "K":
                                keys((c + 1) % KC, b if c < KC - 1 else b + 1)
                                prev = (task, n + 1)
                            elif task == "V":
                                values(k)
                                prev = (task, b * QB + k)
                            elif task == "R":
                                turn_recips(n - 1)
                                prev = (task, n - 1)
                            elif task == "WO":
                                project_out(b - 1, k)
                                prev = (task, (b - 1) * QB + k)
                            else:
                                norm_turn((b + 1) * QB + k, k)
                                prev = (task, (b + 1) * QB + k)

            def epilogue():
                u = NB * UNITS
                for v in range(LAG):
                    turn_probs(u - LAG + v, (v - LAG) % 4, UNITS - LAG + v)
                freed("R", NB - 2)
                turn_recips(NB - 1)
                values_of(NB - 1, KC - 1, B - 1)
                freed("R", NB - 1)
                for i in range(QB):
                    if i:
                        freed("WO", (B - 1) * QB + i - 1)
                    project_out(B - 1, i)

            over_batches(pe, body, epilogue)

            def turn_block(t, i, src, ok, done, hi):
                pe.wait_ge(s[ok], t + 1)
                if some(t):
                    pe.wait_ge(s[hi], t)
                if some(t):
                    pe.wait_ge(s[hi.replace("hi", "lo")], t)
                for k in range(KC):
                    mm = pe.transpose(h_ps[:, k * P:(k + 1) * P], src[:, k * P:(k + 1) * P], ident[:])
                mm.then_inc(s[done], 1)

            pe.wait_ge(s["x1_ok"], B * QB)
            turn_block(0, 0, xb[0], "hn_ok", "hT_mm", "hT_hi")
            pe.wait_ge(s["sel_ok"], BIAS_PARTS)
            pe.wait_ge(s["bias_put"], 16 * BIAS_PARTS)

            def route(t, i, more, loading):
                pe.wait_ge(s["hT_hi"], t + 1)
                pe.wait_ge(s["hT_lo"], t + 1)
                for e in range(NE):
                    if loading:
                        pe.wait_ge(s["fw_hi"], e + 1)
                        pe.wait_ge(s["fw_lo"], e + 1)
                    if some(t * NE + e - 3):
                        pe.wait_ge(s["lg_ok"], t * NE + e - 3)
                    bank = l_ps[e % 4]
                    pe.matmul(bank[:], bias_sel[:, e, :], bias_rows[:], start=True, stop=False)
                    for k in range(KC):
                        mm = three(pe, bank[:], hT_h[i][:, k, :], hT_l[i][:, k, :], w_h[:, e, k, :], w_l[:, e, k, :],
                                   False, k == KC - 1)
                    mm.then_inc(s["lg_mm"], 1)
                    if e == 3 and more:
                        turn_block(t + 1, 1 - i, xb[1 - i], "hn_ok", "hT_mm", "hT_hi")

            route(0, 0, True, True)
            route(1, 1, True, False)
            with pe.Fori(1, NT // 2 - 1) as pair:
                t = pair * 2
                for i in range(2):
                    route(t + i, i, True, False)
            route(NT - 2, 0, True, False)
            route(NT - 1, 1, False, False)

            def turn_c(t, i):
                pe.wait_ge(s["c_put"], t + 1)
                if some(t):
                    pe.wait_ge(s["cT_ok"], t)
                pe.transpose(c_ps[:, 0:P], c_pad[i][:], ident[:]).then_inc(s["cT_mm"], 1)

            def experts(t, i, more, loading):
                pe.wait_ge(s["eT_hi"], t + 1)
                pe.wait_ge(s["eT_lo"], t + 1)
                pe.wait_ge(s["cT_ok"], t + 1)
                if some((t - 1) * (NE + 1) + 1):
                    pe.wait_ge(s["acc"], (t - 1) * (NE + 1) + 1)
                pe.matmul(b_ps[:], cT[i][:], eb[:], start=True, stop=True).then_inc(s["cb_mm"], 1)
                for e in range(NE):
                    if loading:
                        pe.wait_ge(s["ew_hi"], e + 1)
                        pe.wait_ge(s["ew_lo"], e + 1)
                    if e >= 4:
                        pe.wait_ge(s["acc"], t * (NE + 1) + e - 2)
                    else:
                        if some(t * (NE + 1) + e - 3):
                            pe.wait_ge(s["acc"], t * (NE + 1) + e - 3)
                    for k in range(KC):
                        mm = three(pe, l_ps[e % 4][:], hT_h[i][:, k, :], hT_l[i][:, k, :], w_h[:, e, k, :],
                                   w_l[:, e, k, :], k == 0, k == KC - 1)
                    mm.then_inc(s["y_mm"], 1)
                    if e == 3 and more:
                        turn_block(t + 1, 1 - i, hn, "en_ok", "eT_mm", "eT_hi")
                        turn_c(t + 1, 1 - i)

            pe.wait_ge(s["lg_ok"], NT * NE)
            turn_block(0, 0, hn, "en_ok", "eT_mm", "eT_hi")
            pe.wait_ge(s["first_step"], NT * FIRSTS)
            turn_c(0, 0)
            pe.wait_ge(s["eb_in"], 16)
            experts(0, 0, True, True)
            experts(1, 1, True, False)
            with pe.Fori(1, NT // 2 - 1) as pair:
                t = pair * 2
                for i in range(2):
                    experts(t + i, i, True, False)
            experts(NT - 2, 0, True, False)
            experts(NT - 1, 1, False, False)

        @block.scalar
        def _(act):
            act.wait_ge(s["w_in"], 48)
            for dst, src in ((wq_h, wq_raw), (wkv_h, wkv_raw), (wo_h, wo_raw)):
                act.activation(dst[:], src[:], ACT.Copy).then_inc(s["w_hi"], 1)

            def turned_tokens(g, i):
                act.wait_ge(s["xT_mm"], g + 1)
                act.activation(xnT_h[:, :, i * P:(i + 1) * P], j_ps[:].rearrange("p (k q) -> p k q", k=KC), ACT.Copy)\
                    .then_inc(s["xT_hi"], 1)

            def hi_of(n, part, name):
                act.wait_ge(s[name + "_mm"], n + 1)
                if some(n * (16 * STACK_DMAS)):
                    act.wait_ge(s["stacked"], n * (16 * STACK_DMAS))
                act.activation(qk[:, part], j_ps[:], ACT.Copy).then_inc(s[name + "_hi"], 1)

            def copy_probs(u, n, v):
                i, hh = v // 2, 2 * (v % 2)
                act.wait_ge(s["turned"], u * 2 + 1)
                if some(n):
                    act.wait_ge(s["pv"], n)
                act.activation(pT[:, hh, 0:i + 1, i * P:(i + 1) * P],
                               t_ps[0][:, 0:(i + 1) * P].rearrange("p (k q) -> p k q", q=P), ACT.Copy)\
                    .then_inc(s["pt_act"], 1)

            for i in range(QB):
                turned_tokens(i, i)
            hi_of(0, KH, "k")
            hi_of(0, QH, "q")

            def body(b, first, last):
                for c in range(KC):
                    n = b * KC + c
                    for v in range(UNITS):
                        u = n * UNITS + v
                        i, slot, k = v // 2, v % 2, v % 4
                        w = (i + 1) * P
                        db, cc, vv = before(c, v)
                        if not (first and db < 0):
                            copy_probs(u - LAG, n if v >= LAG else n - 1, vv)
                        act.wait_ge(s["negmax"], u + 1)
                        if some((u - 3) * 2):
                            act.wait_ge(s["turned"], (u - 3) * 2)
                        if v == 0:
                            if some(n - 1):
                                act.wait_ge(s["recips"], n - 1)
                        for j in range(2):
                            hh = 2 * (v % 2) + j
                            e = act.activation(probs[:, k, j, 0:w], s_ps[2 * slot + j][:, 0:w], ACT.Exp,
                                               bias=nmax[:, k, j:j + 1], scale=SCALE,
                                               accum_out=sums[:, c % 2, i, hh:hh + 1])
                        e.then_inc(s["exps"], 1)
                        for task, a in fillers(c, v, first, last):
                            if task == "Q":
                                hi_of(n + 1, QH, "q")
                            elif task == "K":
                                hi_of(n + 1, KH, "k")
                            elif task == "V":
                                act.wait_ge(s["v_mm"], b * QB + a + 1)
                                if some(b * KC):
                                    act.wait_ge(s["pv"], b * KC)
                                act.activation(v_sb[:, a, :], j_ps[:], ACT.Copy).then_inc(s["v_ok"], 1)
                            elif task == "R":
                                act.wait_ge(s["r_mm"], n)
                                if some(n - 1):
                                    act.wait_ge(s["o_ok"], n - 1)
                                act.activation(r_sb[:], j_ps[:], ACT.Copy).then_inc(s["r_ok"], 1)
                            elif task == "LNT":
                                turned_tokens((b + 1) * QB + a, a)

            def epilogue():
                for v in range(LAG):
                    copy_probs(NB * UNITS - LAG + v, NB - 1, UNITS - LAG + v)
                act.wait_ge(s["r_mm"], NB)
                act.wait_ge(s["o_ok"], NB - 1)
                act.activation(r_sb[:], j_ps[:], ACT.Copy).then_inc(s["r_ok"], 1)

            over_batches(act, body, epilogue)

            def hi_block(t, i, mm, used, hi):
                act.wait_ge(s[mm], t + 1)
                if some((t - 1) * NE):
                    act.wait_ge(s[used], (t - 1) * NE)
                act.activation(hT_h[i][:], h_ps[:].rearrange("p (k q) -> p k q", k=KC), ACT.Copy)\
                    .then_inc(s[hi], 1)

            hi_block(0, 0, "hT_mm", "lg_mm", "hT_hi")
            for e in range(NE):
                act.wait_ge(s[f"raw{e}_in"], 16)
                act.activation(w_h[:, e], w_raw[:, e], ACT.Copy).then_inc(s["fw_hi"], 1)

            def firsts(t, i, e):
                at = t * FIRSTS + e * 3
                if e == 0:
                    if some(t - 1):
                        act.wait_ge(s["c_ok"], t - 1)
                for j in range(2):
                    if some(at - 2 * (1 - j)):
                        act.wait_ge(s["first_step"], at - 2 * (1 - j))
                    act.wait_ge(s["u_ok"], t * NE + e + j + 1)
                    act.activation(over[j][:], logits[i][:, e + j, :], ACT.Relu).then_inc(s["first_step"], 1)
                for j in range(2):
                    act.wait_ge(s["first_step"], at + 1 + j)
                    act.activation(junk[:], over[j][:], ACT.Sign, accum_out=sign_sum[:, i, e + j:e + j + 1])\
                        .then_inc(s["first_step"], 1)
                    act.wait_ge(s["first_step"], at + 3 + 2 * j)
                    act.activation(over[j][:], over[j][:], ACT.Tanh, scale=0.5,
                                   accum_out=tanh_sum[:, i, e + j:e + j + 1]).then_inc(s["first_step"], 1)

            def tanh_gap(t, i):
                act.wait_ge(s["gap_ok"], t + 1)
                if some(t):
                    act.wait_ge(s["w2_ok"], t)
                if some(t - 1):
                    act.wait_ge(s["c_ok"], t - 1)
                act.activation(th[:], gap[:], ACT.Tanh, scale=0.5, accum_out=th_sum[:, i:i + 1])\
                    .then_inc(s["th_ok"], 1)

            def route(t, i, more, behind=2):
                for e in range(NE):
                    if some(t - 1):
                        act.wait_ge(s["count"], (t - 2) * COUNTS + min(e + 2, COUNTS))
                        act.wait_ge(s["first_step"], (t - 2) * FIRSTS + (FIRSTS * 3 // 4 if e < 6 else FIRSTS))
                    act.wait_ge(s["lg_mm"], t * NE + e + 1)
                    act.activation(logits[i][:, e, :], l_ps[e % 4][:], ACT.Copy).then_inc(s["lg_ok"], 1)
                    if e == 0 and behind >= 2:
                        firsts(t - 2, i, 6)
                    if e == 3 and more:
                        hi_block(t + 1, 1 - i, "hT_mm", "lg_mm", "hT_hi")
                    if e == 3 and behind:
                        tanh_gap(t - 1, 1 - i)
                    if e in (4, 5, 7) and behind:
                        firsts(t - 1, 1 - i, (4, 5, 7).index(e) * 2)

            route(0, 0, True, 0)
            route(1, 1, True, 1)
            with act.Fori(1, NT // 2 - 1) as pair:
                t = pair * 2
                for i in range(2):
                    route(t + i, i, True)
            route(NT - 2, 0, True)
            route(NT - 1, 1, False)
            firsts(NT - 2, 0, 6)
            tanh_gap(NT - 1, 1)
            for e in range(0, NE, 2):
                firsts(NT - 1, 1, e)

            for e in range(NE):
                act.wait_ge(s[f"raw{e}_in"], 32)
                act.activation(w_h[:, e], w_raw[:, e], ACT.Copy).then_inc(s["ew_hi"], 1)
                if e == 0:
                    hi_block(0, 0, "eT_mm", "y_mm", "eT_hi")
                    act.wait_ge(s["cT_mm"], 1)
                    act.activation(cT[0][:], c_ps[:, 0:P], ACT.Copy).then_inc(s["cT_ok"], 1)

            def experts(t, i):
                hi_block(t + 1, 1 - i, "eT_mm", "y_mm", "eT_hi")
                act.wait_ge(s["cT_mm"], t + 2)
                if some(t):
                    act.wait_ge(s["cb_mm"], t)
                act.activation(cT[1 - i][:], c_ps[:, 0:P], ACT.Copy).then_inc(s["cT_ok"], 1)

            experts(0, 0)
            experts(1, 1)
            with act.Fori(1, NT // 2 - 1) as pair:
                t = pair * 2
                for i in range(2):
                    experts(t + i, i)
            experts(NT - 2, 0)

        @block.vector
        def _(dve):
            def statistics(g, slot, src, name):
                dve.bn_stats(stats[:, slot, :], src).then_inc(s[name + "_st"], 1)
                dve.wait_ge(s[name + "_st"], g + 1)
                if some((g - 1) * 2):
                    dve.wait_ge(s[name + "_rs"], (g - 1) * 2)
                dve.memset(turn[:], 0.0)
                dve.bn_aggr(moments[:, slot, :], stats[:, slot, :]).then_inc(s[name + "_var"], 1)

            def normed(g, slot, src, dst, name, ok):
                dve.wait_ge(s[name + "_rs"], (g + 1) * 2)
                dve.tensor_scalar(dst, src, moments[:, slot, 0:1], rstd[:, slot:slot + 1], ALU.subtract, ALU.mult)\
                    .then_inc(s[ok], 1)

            for k, (dst, src, hi) in enumerate(((wq_l, wq_raw, wq_h), (wkv_l, wkv_raw, wkv_h), (wo_l, wo_raw, wo_h))):
                dve.wait_ge(s["w_hi"], k + 1)
                dve.tensor_tensor(dst[:], src[:], f32(hi[:]), ALU.subtract).then_inc(s["w_lo"], 1)

            def block_statistics(b, i):
                if i == 0:
                    dve.wait_ge(s["x_in"], (b + 1) * 16)
                statistics(b * QB + i, i % 2, xt[:, i, :], "ln")

            def norm_block(b, i):
                if some(b * QB + i - 1):
                    dve.wait_ge(s["xT_mm"], b * QB + i - 1)
                normed(b * QB + i, i % 2, xt[:, i, :], xn[:, i % 2, :], "ln", "xn_ok")

            def turned_tokens(g, i):
                dve.wait_ge(s["xT_hi"], g + 1)
                cols = slice(i * P, (i + 1) * P)
                dve.tensor_tensor(xnT_l[:, :, cols], j_ps[:].rearrange("p (k q) -> p k q", k=KC),
                                  f32(xnT_h[:, :, cols]), ALU.subtract).then_inc(s["xT_lo"], 1)

            def lo_of(n, part, name):
                dve.wait_ge(s[name + "_hi"], n + 1)
                dve.tensor_tensor(qk[:, part], j_ps[:], f32(qk[:, part - 1]), ALU.subtract)\
                    .then_inc(s[name + "_lo"], 1)

            def copy_probs(u, n, v):
                i, hh = v // 2, 2 * (v % 2) + 1
                dve.wait_ge(s["turned"], u * 2 + 2)
                if some(n):
                    dve.wait_ge(s["pv"], n)
                dve.tensor_copy(pT[:, hh, 0:i + 1, i * P:(i + 1) * P],
                                t_ps[1][:, 0:(i + 1) * P].rearrange("p (k q) -> p k q", q=P)).then_inc(s["pt_dve"], 1)

            def reciprocals(n, c):
                dve.wait_ge(s["exps"], (n + 1) * UNITS)
                dve.reciprocal(recip[:], sums[:, c % 2]).then_inc(s["recips"], 1)
                dve.wait_ge(s["recips"], n + 1)
                if some(n):
                    dve.wait_ge(s["r_mm"], n)
                dve.tensor_copy(r_rep[:], recip[:].unsqueeze(3).broadcast_to([P, QB, HC, HD])).then_inc(s["reps"], 1)

            def scaled(n):
                dve.wait_ge(s["pv"], n + 1)
                dve.wait_ge(s["r_ok"], n + 1)
                if some(n):
                    dve.wait_ge(s["o_lo"], n)
                dve.tensor_tensor(o_sb[:], o_ps[:], r_sb[:], ALU.mult).then_inc(s["o_ok"], 1)

            def residual(b, i):
                if i == 0:
                    dve.wait_ge(s["xr_in"], (b + 1) * 16)
                dve.wait_ge(s["wo_mm"], b * QB + i + 1)
                dve.tensor_tensor(xr[:, i, :], j_ps[:], xr[:, i, :], ALU.add).then_inc(s["x1_ok"], 1)

            for i in range(QB):
                block_statistics(0, i)
                if i >= 2:
                    turned_tokens(i - 2, i - 2)
                norm_block(0, i)
            turned_tokens(2, 2)
            turned_tokens(3, 3)
            lo_of(0, KL, "k")
            lo_of(0, QL, "q")

            def body(b, first, last):
                for c in range(KC):
                    n = b * KC + c
                    for v in range(UNITS):
                        u = n * UNITS + v
                        i, slot, k = v // 2, v % 2, v % 4
                        w = (i + 1) * P
                        dve.wait_ge(s["scores"], u + 1)
                        for j in range(2):
                            m = dve.tensor_reduce(rmax[:, k, j:j + 1], s_ps[2 * slot + j][:, 0:w], AX_X, ALU.max)
                        m.then_inc(s["rowmax"], 1)
                        dve.wait_ge(s["rowmax"], u + 1)
                        if some(u - 3):
                            dve.wait_ge(s["exps"], u - 3)
                        dve.tensor_scalar(nmax[:, k, :], rmax[:, k, :], -SCALE, None, ALU.mult)\
                            .then_inc(s["negmax"], 1)
                        db, cc, vv = before(c, v)
                        if not (first and db < 0):
                            copy_probs(u - LAG, n if v >= LAG else n - 1, vv)
                        if v == 1 and not (first and c == 0):
                            reciprocals(n - 1, (c - 1) % KC)
                        for task, a in fillers(c, v, first, last):
                            if task == "Q":
                                lo_of(n + 1, QL, "q")
                            elif task == "K":
                                lo_of(n + 1, KL, "k")
                            elif task == "WO":
                                residual(b - 1, a)
                            elif task == "LNT":
                                turned_tokens((b + 1) * QB + a, a)
                        if v == 3 and not (first and c == 0):
                            scaled(n - 1)
                        if c == 2 and 1 <= v < 1 + QB and not last:
                            block_statistics(b + 1, v - 1)
                        if c == 2 and 2 <= v < 2 + QB and not last:
                            norm_block(b + 1, v - 2)

            def epilogue():
                for v in range(LAG):
                    copy_probs(NB * UNITS - LAG + v, NB - 1, UNITS - LAG + v)
                reciprocals(NB - 1, KC - 1)
                scaled(NB - 1)
                for i in range(QB):
                    residual(B - 1, i)

            over_batches(dve, body, epilogue)

            def lo_block(t, i, hi, lo):
                dve.wait_ge(s[hi], t + 1)
                dve.tensor_tensor(hT_l[i][:], h_ps[:].rearrange("p (k q) -> p k q", k=KC), f32(hT_h[i][:]),
                                  ALU.subtract).then_inc(s[lo], 1)

            def stats2(t, i):
                dve.wait_ge(s["xb_in"], (t + 1) * 16)
                statistics(t, i, xb[i][:], "ln2")

            def norm2(t, i):
                normed(t, i, xb[i][:], xb[i][:], "ln2", "hn_ok")

            dve.wait_ge(s["x1_out"], B * 16)
            dve.memset(bias_rows[:], 0.0).then_inc(s["bias_zero"], 1)
            stats2(0, 0)
            norm2(0, 0)
            lo_block(0, 0, "hT_hi", "hT_lo")
            dve.wait_ge(s["bias_in"], 16)
            rows = slice(0, NE)
            dve.tensor_copy(taken[rows, 0, :], bias_raw[rows, :]).then_inc(s["bias_split"], 1)
            dve.wait_ge(s["bias_split"], 1)
            dve.tensor_tensor(bias_rest[rows, :], bias_raw[rows, :], taken[rows, 0, :], ALU.subtract)\
                .then_inc(s["bias_rest_ok"], 1)
            dve.wait_ge(s["bias_rest_ok"], 1)
            dve.tensor_copy(taken[rows, 1, :], bias_rest[rows, :]).then_inc(s["bias_split"], 1)
            dve.wait_ge(s["bias_split"], 2)
            dve.tensor_tensor(taken[rows, 2, :], bias_rest[rows, :], taken[rows, 1, :], ALU.subtract)\
                .then_inc(s["bias_split"], 1)
            for e in range(NE):
                dve.wait_ge(s["fw_hi"], e + 1)
                dve.tensor_tensor(w_l[:, e], w_raw[:, e], f32(w_h[:, e]), ALU.subtract).then_inc(s["fw_lo"], 1)
            stats2(1, 1)
            norm2(1, 1)
            dve.wait_ge(s["bias_put"], 16 * BIAS_PARTS)

            STEPS = 7

            def top_two(t, i, ahead=False):
                lg = logits[i]
                at = t * STEPS
                dve.wait_ge(s["lg_ok"], (t + 1) * NE)
                dve.tensor_tensor(top_a[:], lg[:, 0:4], lg[:, 4:8], ALU.max)
                dve.tensor_tensor(top_b[:], lg[:, 0:4], lg[:, 4:8], ALU.min).then_inc(s["top"], 1)
                if ahead:
                    norm2(t + 2, i)
                dve.wait_ge(s["top"], at + 1)
                if some(t * COUNTS):
                    dve.wait_ge(s["c_sum"], t * COUNTS)
                dve.tensor_tensor(top_c[:], top_a[:, 0:2], top_a[:, 2:4], ALU.max)
                dve.tensor_tensor(top_b[:, 0:2], top_b[:, 0:2], top_b[:, 2:4], ALU.max).then_inc(s["top"], 1)
                dve.tensor_tensor(top_a[:, 0:2], top_a[:, 0:2], top_a[:, 2:4], ALU.min).then_inc(s["top"], 1)
                dve.wait_ge(s["top"], at + 3)
                dve.tensor_tensor(top_b[:, 0:2], top_b[:, 0:2], top_a[:, 0:2], ALU.max).then_inc(s["top"], 1)
                dve.tensor_tensor(top_a[:, 3], top_c[:, 0], top_c[:, 1], ALU.min).then_inc(s["top"], 1)
                dve.tensor_tensor(top_a[:, 2], top_c[:, 0], top_c[:, 1], ALU.max).then_inc(s["top"], 1)
                dve.wait_ge(s["top"], at + 4)
                dve.tensor_tensor(top_b[:, 2], top_b[:, 0], top_b[:, 1], ALU.max).then_inc(s["top"], 1)
                dve.wait_ge(s["top"], at + 7)
                if some(t):
                    dve.wait_ge(s["u_ok"], t * NE)
                dve.tensor_tensor(second[:], top_a[:, 3], top_b[:, 2], ALU.max).then_inc(s["second_ok"], 1)
                dve.wait_ge(s["second_ok"], t + 1)
                if some(t):
                    dve.wait_ge(s["th_ok"], t)
                dve.tensor_tensor(gap[:], top_a[:, 2], second[:], ALU.subtract).then_inc(s["gap_ok"], 1)
                dve.wait_ge(s["gap_ok"], t + 1)
                dve.scalar_tensor_tensor(taken[:, 0, :], gap[:], 0.0, minus_one[:].broadcast_to([P, O]), ALU.is_equal,
                                         ALU.mult, accum_out=c_taken[:, i, 0:1]).then_inc(s["count"], 1)

            def weigh(t, i, between=None):
                lg = logits[i]
                at = t * COUNTS
                dve.wait_ge(s["th_ok"], t + 1)
                dve.tensor_scalar(w2[:], th[:], -0.5, 0.5, ALU.mult, ALU.add).then_inc(s["w2_ok"], 1)
                dve.wait_ge(s["w2_ok"], t + 1)
                dve.wait_ge(s["count"], at + 1)
                dve.tensor_scalar(c_taken[:, i, 0:1], c_taken[:, i, 0:1], 0.5, None, ALU.mult)\
                    .then_inc(s["c_sum"], 1)
                for e in range(NE):
                    if between is not None:
                        between(e)
                    if e < NE - 1:
                        dve.wait_ge(s["u_ok"], t * NE + e + 1)
                        dve.wait_ge(s["count"], at + e + 1)
                        dve.scalar_tensor_tensor(taken[:, (e + 1) % 3, :], lg[:, e, :], 0.0, taken[:, e % 3, :],
                                                 ALU.is_equal, ALU.add).then_inc(s["count"], 1)
                    else:
                        dve.wait_ge(s["count"], at + e + 1)
                    if e:
                        dve.scalar_tensor_tensor(scrap[:, e % 2, :], taken[:, e % 3, :], 1.0, w2[:], ALU.min,
                                                 ALU.mult, accum_out=c_taken[:, i, e:e + 1]).then_inc(s["c_sum"], 1)

            def finish_c(t, i):
                dve.tensor_scalar(c_taken[:, i, NE:NE + 1], th_sum[:, i:i + 1], -0.5, 0.5 * O, ALU.mult, ALU.add)\
                    .then_inc(s["c_half"], 1)
                dve.wait_ge(s["first_step"], (t + 1) * FIRSTS)
                dve.tensor_tensor(c_first[:], tanh_sum[:, i, :], sign_sum[:, i, :], ALU.add).then_inc(s["c_half"], 1)
                dve.wait_ge(s["c_half"], t * 3 + 1)
                dve.tensor_tensor(c_diff[:], c_taken[:, i, 1:NE + 1], c_taken[:, i, 0:NE], ALU.subtract)\
                    .then_inc(s["c_half"], 1)
                dve.wait_ge(s["c_half"], (t + 1) * 3)
                dve.scalar_tensor_tensor(c_all[:, bass.ds(t, 1), :].rearrange("p a e -> p (a e)"), c_first[:], 0.5,
                                         c_diff[:], ALU.mult, ALU.add).then_inc(s["c_ok"], 1)

            def route(t, i, ahead, behind=True):
                if ahead:
                    stats2(t + 2, i)
                top_two(t, i, ahead)
                if ahead:
                    lo_block(t + 2, i, "hT_hi", "hT_lo")
                if behind:
                    finish_c(t - 1, 1 - i)
                weigh(t, i)

            lo_block(1, 1, "hT_hi", "hT_lo")
            route(0, 0, True, False)
            route(1, 1, True)
            with dve.Fori(1, NT // 2 - 1) as pair:
                t = pair * 2
                for i in range(2):
                    route(t + i, i, True)
            route(NT - 2, 0, False)
            top_two(NT - 1, 1)
            dve.wait_ge(s["c_sum"], (NT - 1) * COUNTS)
            finish_c(NT - 2, 0)

            def norm3(t, i):
                dve.wait_ge(s["xe_in"], (t + 1) * 16)
                statistics(t, i, xb[i][:], "ln3")
                if some(t):
                    dve.wait_ge(s["eT_mm"], t)
                normed(t, i, xb[i][:], hn[:], "ln3", "en_ok")

            def put_c(t, i):
                if some(t - 1):
                    dve.wait_ge(s["cT_mm"], t - 1)
                dve.tensor_copy(c_pad[i][:, 0:NE], c_all[:, bass.ds(t, 1), :].rearrange("p a e -> p (a e)"))\
                    .then_inc(s["c_put"], 1)

            norm3(0, 0)
            dve.wait_ge(s["pad_z"], 3)
            put_c(0, 0)
            lo_block(0, 0, "eT_hi", "eT_lo")

            def lo_weight(e):
                dve.wait_ge(s["ew_hi"], e + 1)
                dve.tensor_tensor(w_l[:, e], w_raw[:, e], f32(w_h[:, e]), ALU.subtract).then_inc(s["ew_lo"], 1)

            weigh(NT - 1, 1, lo_weight)
            dve.wait_ge(s["c_sum"], NT * COUNTS)
            finish_c(NT - 1, 1)

            def experts(t, i, more):
                dve.wait_ge(s["cb_mm"], t + 1)
                dve.tensor_tensor(xb[i][:], b_ps[:], xb[i][:], ALU.add).then_inc(s["acc"], 1)
                for e in range(NE):
                    dve.wait_ge(s["y_mm"], t * NE + e + 1)
                    dve.wait_ge(s["acc"], t * (NE + 1) + e + 1)
                    dve.scalar_tensor_tensor(xb[i][:], l_ps[e % 4][:], c_pad[i][:, e:e + 1], xb[i][:], ALU.mult,
                                             ALU.add).then_inc(s["acc"], 1)
                    if more and e == 2:
                        norm3(t + 1, 1 - i)
                        put_c(t + 1, 1 - i)
                    if more and e == 3:
                        lo_block(t + 1, 1 - i, "eT_hi", "eT_lo")

            experts(0, 0, True)
            experts(1, 1, True)
            with dve.Fori(1, NT // 2 - 1) as pair:
                t = pair * 2
                for i in range(2):
                    experts(t + i, i, True)
            experts(NT - 2, 0, True)
            experts(NT - 1, 1, False)

        @block.gpsimd
        def _(pool):
            pool.memset(ident[:], 0.0).then_inc(s["const_z"], 1)
            pool.memset(identb[:], 0.0).then_inc(s["const_z"], 1)
            pool.memset(maskb[:], 0.0).then_inc(s["const_z"], 1)
            pool.memset(minus_half[:], -0.5).then_inc(s["const_z"], 1)
            pool.memset(minus_one[:], -1.0).then_inc(s["const_z"], 1)
            pool.memset(eps[:], EPS).then_inc(s["const_z"], 1)
            pool.memset(zero[:], 0.0).then_inc(s["const_z"], 1)
            pool.wait_ge(s["const_z"], 7)
            for m in (ident, identb):
                pool.affine_select(out=m[:], in_=m[:], compare_op=ALU.not_equal, fill=1.0, base=0,
                                   pattern=[[-1, P]], channel_multiplier=1).then_inc(s["const_one"], 1)
            pool.affine_select(out=maskb[:], in_=maskb[:], compare_op=ALU.is_ge, fill=MASKED, base=0,
                               pattern=[[-1, P]], channel_multiplier=1).then_inc(s["const_mask"], 1)

            def split_context(b):
                pool.wait_ge(s["ctx_in"], (b + 1) * 16)
                if some(b * KC):
                    pool.wait_ge(s["k_mm"], b * KC)
                pool.tensor_tensor(ctx_h[:], ctx_raw[:], zero[:].broadcast_to([P, S]), ALU.add).then_inc(s["ctx_split"], 1)
                pool.wait_ge(s["ctx_split"], b * 2 + 1)
                pool.tensor_tensor(ctx_l[:], ctx_raw[:], f32(ctx_h[:]), ALU.subtract).then_inc(s["ctx_split"], 1)

            def split_outputs(n, c, b):
                pool.wait_ge(s["o_ok"], n + 1)
                if c == 0:
                    if some(b * QB):
                        pool.wait_ge(s["wo_mm"], b * QB)
                pool.tensor_tensor(oT_h[:, c, :], o_sb[:], zero[:].broadcast_to([P, S]), ALU.add).then_inc(s["o_hi"], 1)
                pool.wait_ge(s["o_hi"], n + 1)
                pool.tensor_tensor(oT_l[:, c, :], o_sb[:], f32(oT_h[:, c, :]), ALU.subtract).then_inc(s["o_lo"], 1)

            def deviation(g, slot, name):
                pool.wait_ge(s[name + "_var"], g + 1)
                if some(g - 1):
                    pool.wait_ge(s[{"ln": "xn_ok", "ln2": "hn_ok", "ln3": "en_ok"}[name]], g - 1)
                r = rstd[:, slot:slot + 1]
                pool.tensor_tensor(r, moments[:, slot, 1:2], eps[:], ALU.add).then_inc(s[name + "_rs"], 1)
                pool.wait_ge(s[name + "_rs"], g * 2 + 1)
                pool.tensor_tensor(r, r, minus_half[:], ALU.pow).then_inc(s[name + "_rs"], 1)

            split_context(0)
            for i in range(QB):
                deviation(i, i % 2, "ln")

            def body(b, first, last):
                for c in range(KC):
                    n = b * KC + c
                    if c == 2 and not last:
                        for i in range(QB):
                            deviation((b + 1) * QB + i, i % 2, "ln")
                    if not (first and c == 0):
                        split_outputs(n - 1, (c - 1) % KC, b if c else b - 1)
                    if c == 2 and not last:
                        split_context(b + 1)

            def epilogue():
                split_outputs(NB - 1, KC - 1, B - 1)

            over_batches(pool, body, epilogue)

            pool.wait_ge(s["x1_out"], B * 16)
            pool.memset(bias_sel[:], 0.0).then_inc(s["sel_z"], 1)
            pool.wait_ge(s["sel_z"], 1)
            for k in range(BIAS_PARTS):
                if some(k):
                    pool.wait_ge(s["sel_ok"], k)
                pool.affine_select(out=bias_sel[:], in_=bias_sel[:], compare_op=ALU.not_equal, fill=1.0,
                                   base=-k * NE, pattern=[[-1, NE], [0, P]], channel_multiplier=1)\
                    .then_inc(s["sel_ok"], 1)

            def less_second(t, i):
                pool.wait_ge(s["second_ok"], t + 1)
                for e in range(NE):
                    pool.tensor_tensor(logits[i][:, e, :], logits[i][:, e, :], second[:], ALU.subtract)\
                        .then_inc(s["u_ok"], 1)

            deviation(0, 0, "ln2")
            deviation(1, 1, "ln2")
            with pool.Fori(0, NT // 2 - 1) as pair:
                t = pair * 2
                for i in range(2):
                    deviation(t + i + 2, i, "ln2")
                    less_second(t + i, i)
            less_second(NT - 2, 0)
            less_second(NT - 1, 1)

            pool.wait_ge(s["c_ok"], NT - 1)
            for m in (eb, c_pad[0], c_pad[1]):
                pool.memset(m[:], 0.0).then_inc(s["pad_z"], 1)
            deviation(0, 0, "ln3")
            deviation(1, 1, "ln3")
            with pool.Fori(1, NT // 2) as pair:
                t = pair * 2
                for i in range(2):
                    deviation(t + i, i, "ln3")


_OUT = "out_0_dram"


def kernel(x, ctx_512, L0_xattn_Wq, L0_xattn_Wkv_expand, L0_xattn_Wout, L0_ffn_router_w, L0_ffn_router_b,
           L0_ffn_expert_w, L0_ffn_expert_b):
    import numpy as np
    import concourse.bacc as bacc
    from concourse.bass_utils import run_bass_kernel_spmd

    arrays = {
        "x": np.asarray(x).reshape(B * S, H),
        "ctxT": np.asarray(ctx_512)[:, :S, :].transpose(0, 2, 1).reshape(B * P, S),
        "wqT": np.asarray(L0_xattn_Wq).T,
        "wkvT": np.asarray(L0_xattn_Wkv_expand).T,
        "woT": np.asarray(L0_xattn_Wout).T,
        "routerT": np.asarray(L0_ffn_router_w).reshape(O, NE, H).transpose(2, 1, 0),
        "router_b": np.asarray(L0_ffn_router_b).reshape(O, NE).T,
        "expertT": np.asarray(L0_ffn_expert_w).transpose(2, 0, 1),
        "expert_b": np.asarray(L0_ffn_expert_b),
    }
    arrays = {f"in_{n}": np.ascontiguousarray(a) for n, a in arrays.items()}
    nc = bacc.Bacc("TRN2", target_bir_lowering=False, num_devices=1)
    args = [nc.dram_tensor(n, a.shape, mybir.dt.from_np(a.dtype), kind="ExternalInput").ap()
            for n, a in arrays.items()]
    out = nc.dram_tensor(_OUT, (B * S, H), F32, kind="ExternalOutput").ap()
    build(nc, *args, out)
    r = run_bass_kernel_spmd(nc, [arrays], core_ids=[0])
    return np.asarray(r.results[0][_OUT]).reshape(B, S, H)
```

```python
from contextlib import ExitStack

import concourse.bass as bass
from concourse import mybir

ALU = mybir.AluOpType
ACT = mybir.ActivationFunctionType
F32 = mybir.dt.float32
F32R = mybir.dt.float32r
BF16 = mybir.dt.bfloat16
AX_X = mybir.AxisListType.X

P = 128
B, S, H = 8, 512, 512
NH, HD = 16, 32
KC = H // P
QB = S // P
HC = P // HD
NE, O = 8, 512
NT = B * S // P
NB = B * KC
UNITS = QB * 2
LAG = 2
STACK = 3 * HD
STACK_DMAS = 3 * HC
SCALE = float(HD) ** -0.5
EPS = 1e-5
MASKED = -1e30
BIAS_PARTS = 3


def build(nc, x, ctxT, wqT, wkvT, woT, routerT, router_b, expertT, expert_b, out):
    ctx = ExitStack()
    with ctx:
        def sem(name):
            return ctx.enter_context(nc.semaphore(name))

        size = {F32: 4, F32R: 4, BF16: 2}
        start = (nc.sbuf_base + 63) // 64 * 64

        class Place:

            def __init__(self, at):
                self.at = at

            def __call__(self, name, shape, dtype, at=None):
                n = size[dtype]
                for d in shape[1:]:
                    n *= d
                if at is None:
                    at = self.at
                    self.at += (n + 31) // 32 * 32
                assert at + n <= nc.sbuf_usable_end, (name, at + n)
                return nc.alloc_sbuf_tensor_at(name, shape, dtype, offset=at)

        keep = Place(start)
        ident = keep("ident", [P, P], F32)
        identb = keep("identb", [P, P], BF16)
        maskb = keep("maskb", [P, P], BF16)
        c_all = keep("c_all", [P, NT, NE], F32)
        stats = keep("stats", [P, QB, 6], F32)
        moments = keep("moments", [P, QB, 2], F32)
        rstd = keep("rstd", [P, QB], F32)
        minus_one = keep("minus_one", [P, 1], F32)
        minus_half = keep("minus_half", [P, 1], F32)
        eps = keep("eps", [P, 1], F32)
        zero = keep("zero", [P, 1], F32)
        turn = keep("turn", [P, 1], F32)

        att = Place(keep.at)
        wq_h = att("wq_h", [P, KC, H], F32R)
        wq_l = att("wq_l", [P, KC, H], F32R)
        wkv_h = att("wkv_h", [P, 2 * H], F32R)
        wkv_l = att("wkv_l", [P, 2 * H], F32R)
        xt = att("xt", [P, QB, H], F32)
        xn = att("xn", [P, 2, H], F32)
        xnT_h = att("xnT_h", [P, KC, S], F32R)
        xnT_l = att("xnT_l", [P, KC, S], F32R)
        ctx_raw = att("ctx_raw", [P, S], F32)
        ctx_h = att("ctx_h", [P, S], F32R)
        ctx_l = att("ctx_l", [P, S], F32R)
        early = (att.at - keep.at) // (4 * KC * O)
        v_sb = att("v_sb", [P, QB, H], F32)
        qk = att("qk", [P, 4, S], F32R)
        QH, QL, KH, KL = range(4)
        qk_st = [att(f"qk_st{i}", [P, HC, 2, S], F32R) for i in range(2)]
        probs = att("probs", [P, 4, 2, S], F32)
        pT_at = att.at
        pT = att("pT", [P, HC, QB, S], F32)
        pT_end = att.at
        r_sb = att("r_sb", [P, S], F32)
        r_rep = att("r_rep", [P, QB, HC, HD], F32)
        recip = att("recip", [P, QB, HC], F32)
        sums = att("sums", [P, 2, QB, HC], F32)
        nmax = att("nmax", [P, 4, 2], F32)
        o_sb = att("o_sb", [P, S], F32)
        oT_h = att("oT_h", [P, KC, S], F32R)
        oT_l = att("oT_l", [P, KC, S], F32R)
        wo_h = att("wo_h", [P, KC, H], F32R)
        wo_l = att("wo_l", [P, KC, H], F32R)
        xr = att("xr", [P, QB, H], F32)
        raw = Place(pT_at)
        wq_raw = raw("wq_raw", [P, KC, H], F32)
        wkv_raw = raw("wkv_raw", [P, 2 * H], F32)
        wo_raw = raw("wo_raw", [P, KC, H], F32)

        ffn = Place(keep.at)
        raw_at = ffn.at
        w_l = ffn("w_l", [P, NE, KC, O], F32R)
        w_raw = ffn("w_raw", [P, NE, KC, O], F32, at=raw_at)
        w_h = ffn("w_h", [P, NE, KC, O], F32R)
        w_h_end = ffn.at
        xb = [ffn(f"xb{i}", [P, H], F32) for i in range(2)]
        hT_h = [ffn(f"hT_h{i}", [P, KC, P], F32R) for i in range(2)]
        hT_l = [ffn(f"hT_l{i}", [P, KC, P], F32R) for i in range(2)]
        bias_sel = ffn("bias_sel", [P, NE, P], BF16)
        bias_rows = ffn("bias_rows", [P, O], BF16)
        logits_at = ffn.at
        logits = [ffn(f"logits{i}", [P, NE, O], F32) for i in range(2)]
        top_a = ffn("top_a", [P, 4, O], F32)
        top_b = ffn("top_b", [P, 4, O], F32)
        second = ffn("second", [P, O], F32)
        gap = ffn("gap", [P, O], F32)
        th = ffn("th", [P, O], F32)
        w2 = ffn("w2", [P, O], F32)
        top_c = ffn("top_c", [P, 2, O], F32, at=ffn.at)
        taken = ffn("taken", [P, 3, O], BF16)
        scrap = ffn("scrap", [P, 2, O], BF16)
        tanh_sum = ffn("tanh_sum", [P, 2, NE], F32)
        th_sum = ffn("th_sum", [P, 2], F32)
        sign_sum = ffn("sign_sum", [P, 2, NE], F32)
        c_first = ffn("c_first", [P, NE], F32)
        c_taken = ffn("c_taken", [P, 2, NE + 1], F32)
        c_diff = ffn("c_diff", [P, NE], F32)
        c_now = [ffn(f"c_now{i}", [P, NE], F32) for i in range(2)]
        c_hi = ffn("c_hi", [P, NE], F32R)
        bias = Place(logits_at)
        bias_raw = bias("bias_raw", [P, O], F32)
        bias_rest = bias("bias_rest", [P, O], F32)
        bias_parts = bias("bias_parts", [P, BIAS_PARTS, O], BF16)
        assert bias.at <= pT_end and w_h_end <= pT_end
        exp_ = Place(logits_at)
        hn = exp_("hn", [P, H], F32)
        eb = exp_("eb", [P, O], F32R)
        eb_raw = exp_("eb_raw", [P, O], F32)
        c_pad = [exp_(f"c_pad{i}", [P, P], F32) for i in range(2)]
        cT = [exp_(f"cT{i}", [P, P], F32R) for i in range(2)]
        assert exp_.at <= logits_at + 4 * NE * O // 2

        x1 = nc.dram_tensor("x1", [NT * P, H], F32, kind="Internal").ap()

        pairs = [ctx.enter_context(nc.psum_tensor(f"pair{i}", [P, 2, 512], F32)) for i in range(2)]
        ps = [ctx.enter_context(nc.psum_tensor(f"ps{i}", [P, 512], F32)) for i in range(4, 8)]
        s_ps = pairs
        t_ps = ps[0:2]
        j_ps = ps[2:4]
        o_ps = j_ps[0]
        l_ps = [pairs[i // 2][:, i % 2, :] for i in range(4)]
        h_ps = ps[0]
        over = [ps[1][:], ps[2][:]]
        junk = ps[3]
        c_ps = ps[2]
        b_ps = ps[1]

        names = """
            const_z const_one const_mask wkv_in wq_in wo_in w_hi w_lo x_in ctx_in ln_st ln_var ln_rs xn_ok xT_mm xT_hi xT_lo ctx_split q_mm q_hi q_lo
            k_mm k_hi k_lo stacked v_mm v_ok scores negmax exps turned pt_act pt_dve pv recips
            reps r_mm r_ok o_ok o_hi o_lo wo_mm x1_ok xr_in x1_out
            fw_hi fw_lo bias_in bias_zero bias_split bias_rest_ok bias_put sel_z sel_ok xb_in ln2_st ln2_var ln2_rs hn_ok
            hT_mm hT_hi hT_lo lg_mm lg_ok top gap_ok th_ok second_ok u_ok w2_ok count first_step c_sum c_half c_ok
            ew_hi ew_lo ew_lo_pool eb_in eb_hi eb_lo c_hi_ok xe_in ln3_st ln3_var ln3_rs en_ok eT_mm eT_hi eT_lo pad_z c_put cT_mm cT_ok cb_mm
            y_mm acc y_out
        """.split()
        names += [f"raw{e}_in" for e in range(NE)]
        s = {n: sem(n) for n in names}

        def some(value):
            return not isinstance(value, int) or value > 0

        POOL_LO = 3
        COUNTS = NE
        FIRSTS = NE * 3

        def f32(ap):
            return ap.bitcast(F32)

        def three(pe, dst, lh, ll, rh, rl, start, stop):
            pe.matmul(dst, lh, rh, start=start, stop=False)
            pe.matmul(dst, lh, rl, start=False, stop=False)
            return pe.matmul(dst, ll, rh, start=False, stop=stop)

        def before(c, v):
            k = c * UNITS + v - LAG
            return (k // (KC * UNITS), k % (KC * UNITS) // UNITS, k % UNITS)

        def fillers(c, v, first, last):
            found = []
            if v == 0 and not (last and c == KC - 1):
                found.append(("K", None))
            if v == 1 and not (last and c == KC - 1):
                found.append(("Q", None))
            if v == 2 and not (first and c == 0):
                found.append(("R", None))
            if c == 0 and v >= 4:
                found.append(("V", v - 4))
            if c == 1 and v >= 4 and not first:
                found.append(("WO", v - 4))
            if c == 2 and v >= 4 and not last:
                found.append(("LNT", v - 4))
            return found

        BANK = {"K": 0, "Q": 1, "PV": 0, "R": 1}

        SLOTS = {"ln": QB, "ln2": 2, "ln3": 2}

        def over_batches(eng, body, epilogue):
            body(0, True, False)
            with eng.Fori(1, B - 1) as b:
                body(b, False, False)
            body(B - 1, False, True)
            epilogue()

        block = ctx.enter_context(nc.Block())

        @block.sync
        def _(sp):
            sp.dma_start(xt[:], x[0:S, :].rearrange("(i p) h -> p i h", p=P)).then_inc(s["x_in"], 16)
            sp.dma_start(ctx_raw[:], ctxT[0:P, :]).then_inc(s["ctx_in"], 16)
            sp.dma_start(wkv_raw[:], wkvT).then_inc(s["wkv_in"], 16)
            sp.dma_start(wq_raw[:], wqT.rearrange("(c p) n -> p c n", p=P)).then_inc(s["wq_in"], 16)
            sp.dma_start(wo_raw[:], woT.rearrange("(c p) n -> p c n", p=P)).then_inc(s["wo_in"], 16)

            def stack(n, par, stored=0):
                sp.wait_ge(s["k_hi"], n + 1)
                sp.wait_ge(s["k_lo"], n + 1)
                sp.wait_ge(s["q_hi"], n + 1)
                sp.wait_ge(s["q_lo"], n + 1)
                for g, (q, k) in enumerate(((QH, KH), (QL, KH), (QH, KL))):
                    if g == 2 and some(stored):
                        sp.wait_ge(s["x1_out"], stored)
                    for hh in range(HC):
                        sp.dma_start(f32(qk_st[par][g * HD:(g + 1) * HD, hh]),
                                     f32(qk[hh * HD:(hh + 1) * HD, q:k + 1:k - q])).then_inc(s["stacked"], 16)

            def tokens(ap, b):
                return ap[bass.ds(b * S, S), :].rearrange("(i p) h -> p i h", p=P)

            def body(b, first, last):
                for c in range(KC):
                    n = b * KC + c
                    if c == 0 and not first:
                        sp.dma_start(xr[:], tokens(x, b - 1)).then_inc(s["xr_in"], 16)
                    if c == 0 and not last:
                        sp.wait_ge(s["xn_ok"], (b + 1) * QB)
                        sp.dma_start(xt[:], tokens(x, b + 1)).then_inc(s["x_in"], 16)
                    if c == 1 and not last:
                        sp.wait_ge(s["ctx_split"], (b + 1) * 2)
                        sp.dma_start(ctx_raw[:], ctxT[bass.ds((b + 1) * P, P), :]).then_inc(s["ctx_in"], 16)
                    if not (last and c == KC - 1):
                        stack(n + 1, (c + 1) % 2, 0 if first or c < KC - 1 else b * 16)
                    if c == 1 and not first:
                        sp.wait_ge(s["x1_ok"], b * QB)
                        sp.dma_start(tokens(x1, b - 1), xr[:]).then_inc(s["x1_out"], 16)

                    if last and c == KC - 2:
                        sp.wait_ge(s["q_mm"], NB)
                        sp.wait_ge(s["k_mm"], NB)
                        for e in range(early):
                            sp.dma_start(w_raw[:, e], r_v[:, e]).then_inc(s[f"raw{e}_in"], 16)

            def load_block(t, i, name):
                if some(t * 16):
                    sp.wait_ge(s[name], t * 16)
                sp.dma_start(xb[i][:], x1[bass.ds(t * P, P), :]).then_inc(s[name], 16)

            def epilogue():
                sp.wait_ge(s["x1_out"], (B - 1) * 16)
                sp.dma_start(xr[:], tokens(x, B - 1)).then_inc(s["xr_in"], 16)
                sp.wait_ge(s["pv"], NB)
                load_block(0, 0, "xb_in")
                sp.dma_start(bias_raw[0:NE, :], router_b).then_inc(s["bias_in"], 16)
                for e in range(early, NE):
                    sp.dma_start(w_raw[:, e], r_v[:, e]).then_inc(s[f"raw{e}_in"], 16)
                load_block(1, 1, "xb_in")
                sp.wait_ge(s["bias_zero"], 1)
                for k in range(BIAS_PARTS):
                    sp.wait_ge(s["bias_split"], k + 1)
                    sp.dma_start(bias_rows[k * NE:(k + 1) * NE, :], bias_parts[0:NE, k, :])\
                        .then_inc(s["bias_put"], 16)
                sp.wait_ge(s["x1_ok"], B * QB)
                sp.dma_start(tokens(x1, B - 1), xr[:]).then_inc(s["x1_out"], 16)
                sp.wait_ge(s["x1_out"], B * 16)

            r_v = routerT.rearrange("(c p) e o -> p e c o", p=P)
            e_v = expertT.rearrange("(c p) e o -> p e c o", p=P)
            stack(0, 0)
            over_batches(sp, body, epilogue)

            def router_pair(t, more):
                for i in range(2):
                    if more:
                        sp.wait_ge(s["hT_mm"], t + i + 1)
                        load_block(t + i + 2, i, "xb_in")

            with sp.Fori(0, NT // 2 - 1) as pair:
                t = pair * 2
                router_pair(t, True)
            sp.wait_ge(s["hT_mm"], NT - 1)
            load_block(0, 0, "xe_in")
            sp.wait_ge(s["hT_mm"], NT)
            load_block(1, 1, "xe_in")
            for e in range(NE):
                sp.wait_ge(s["lg_mm"], (NT - 1) * NE + e + 1)
                sp.dma_start(w_raw[:, e], e_v[:, e]).then_inc(s[f"raw{e}_in"], 16)
            sp.wait_ge(s["pad_z"], 1)
            for g in range(3):
                sp.dma_start(eb_raw[g * HD:g * HD + NE, :], expert_b).then_inc(s["eb_in"], 16)

            def expert_pair(t, more):
                for i in range(2):
                    sp.wait_ge(s["acc"], (t + i + 1) * (NE + 1))
                    sp.dma_start(out[bass.ds((t + i) * P, P), :], xb[i][:]).then_inc(s["y_out"], 16)
                    if more:
                        sp.wait_ge(s["y_out"], (t + i + 1) * 16)
                        load_block(t + i + 2, i, "xe_in")

            with sp.Fori(0, NT // 2 - 1) as pair:
                t = pair * 2
                expert_pair(t, True)
            expert_pair(NT - 2, False)
            sp.wait_ge(s["y_out"], NT * 16)

        @block.tensor
        def _(pe):
            def freed(task, k):
                if task == "PV":
                    if some(k + 1):
                        pe.wait_ge(s["o_ok"], k + 1)
                    return
                for name in {"Q": ("q_hi", "q_lo"), "K": ("k_hi", "k_lo"), "V": ("v_ok",), "R": ("r_ok",),
                             "LNT": ("xT_hi", "xT_lo"), "WO": ("x1_ok",)}[task]:
                    pe.wait_ge(s[name], k + 1)

            def norm_turn(g, i):
                pe.wait_ge(s["xn_ok"], g + 1)
                for k in range(KC):
                    mm = pe.transpose(j_ps[i % 2][:, k * P:(k + 1) * P], xn[:, i % 2, k * P:(k + 1) * P], ident[:])
                mm.then_inc(s["xT_mm"], 1)

            def queries(n, c):
                if c == 0:
                    pe.wait_ge(s["xT_hi"], n + QB)
                    pe.wait_ge(s["xT_lo"], n + QB)
                cols = slice(c * P, (c + 1) * P)
                for k in range(KC):
                    mm = three(pe, j_ps[BANK["Q"]][:], wq_h[:, k, cols], wq_l[:, k, cols], xnT_h[:, k, :], xnT_l[:, k, :],
                               k == 0, k == KC - 1)
                mm.then_inc(s["q_mm"], 1)

            def keys(c, b):
                if c == 0:
                    pe.wait_ge(s["ctx_split"], (b + 1) * 2)
                cols = slice(c * P, (c + 1) * P)
                three(pe, j_ps[BANK["K"]][:], wkv_h[:, cols], wkv_l[:, cols], ctx_h[:], ctx_l[:], True, True)\
                    .then_inc(s["k_mm"], 1)

            def values(kb):
                rows = slice(kb * P, (kb + 1) * P)
                three(pe, j_ps[kb % 2][:], ctx_h[:, rows], ctx_l[:, rows], wkv_h[:, H:2 * H], wkv_l[:, H:2 * H],
                      True, True)\
                    .then_inc(s["v_mm"], 1)

            def turn_recips(n):
                pe.wait_ge(s["reps"], n + 1)
                for i in range(QB):
                    mm = pe.transpose(j_ps[BANK["R"]][:, i * P:(i + 1) * P], r_rep[:, i].rearrange("p a d -> p (a d)"), ident[:])
                mm.then_inc(s["r_mm"], 1)

            def project_out(b, i):
                pe.wait_ge(s["o_hi"], (b + 1) * KC)
                pe.wait_ge(s["o_lo"], (b + 1) * KC)
                rows = slice(i * P, (i + 1) * P)
                for c in range(KC):
                    mm = three(pe, j_ps[i % 2][:], oT_h[:, c, rows], oT_l[:, c, rows], wo_h[:, c, :], wo_l[:, c, :],
                               c == 0, c == KC - 1)
                mm.then_inc(s["wo_mm"], 1)

            def turn_probs(u, k, v):
                pe.wait_ge(s["exps"], u + 1)
                i = v // 2
                for j in range(2):
                    if some(u):
                        pe.wait_ge(s[("pt_act", "pt_dve")[j]], u)
                    for kb in range(i + 1):
                        mm = pe.transpose(t_ps[j][:, kb * P:(kb + 1) * P], probs[:, k, j, kb * P:(kb + 1) * P], ident[:])
                    mm.then_inc(s["turned"], 1)

            def values_of(n, c, b):
                pe.wait_ge(s["pt_act"], (n + 1) * UNITS)
                pe.wait_ge(s["pt_dve"], (n + 1) * UNITS)
                pe.wait_ge(s["v_ok"], (b + 1) * QB)
                for kb in range(QB):
                    for hh in range(HC):
                        h = c * HC + hh
                        mm = pe.matmul(o_ps[hh * HD:(hh + 1) * HD, kb * P:S], v_sb[:, kb, h * HD:(h + 1) * HD],
                                       pT[:, hh, kb, kb * P:S], start=(kb == 0), stop=(kb == QB - 1),
                                       tile_position=(0, hh * HD), skip_group_check=True)
                mm.then_inc(s["pv"], 1)

            pe.wait_ge(s["const_one"], 2)
            for i in range(QB):
                if i >= 2:
                    freed("LNT", i - 2)
                norm_turn(i, i)
            pe.wait_ge(s["w_hi"], 1)
            pe.wait_ge(s["w_lo"], 1)
            freed("LNT", QB - 2)
            keys(0, 0)
            pe.wait_ge(s["w_hi"], 2)
            pe.wait_ge(s["w_lo"], 2)
            freed("LNT", QB - 1)
            queries(0, 0)
            pe.wait_ge(s["w_hi"], 3)
            pe.wait_ge(s["w_lo"], 3)
            pe.wait_ge(s["const_mask"], 1)

            def body(b, first, last):
                held = [("K", 0), ("Q", 0)] if first else [("PV", b * KC - 2), ("R", b * KC - 2)]
                for c in range(KC):
                    n = b * KC + c
                    for v in range(UNITS):
                        u = n * UNITS + v
                        i, slot = v // 2, v % 2
                        w = (i + 1) * P
                        if v == 0:
                            pe.wait_ge(s["stacked"], (n + 1) * (16 * STACK_DMAS))
                        if some(u - 1):
                            pe.wait_ge(s["exps"], u - 1)
                        for j in range(2):
                            hh = 2 * (v % 2) + j
                            bank = s_ps[slot][:, j, :]
                            pe.matmul(bank[:, 0:w], qk_st[c % 2][0:STACK, hh, 0, i * P:w], qk_st[c % 2][0:STACK, hh, 1, 0:w],
                                      start=True, stop=False)
                            mm = pe.matmul(bank[:, i * P:w], identb[:], maskb[:], start=False, stop=True)
                        mm.then_inc(s["scores"], 1)
                        if v == LAG and not (first and c == 0):
                            freed(*held[0])
                            held[0] = ("PV", n - 1)
                            values_of(n - 1, (c - 1) % KC, b if c else b - 1)
                        db, _, vv = before(c, v)
                        if not (first and db < 0):
                            turn_probs(u - LAG, (v - LAG) % 4, vv)
                        for task, k in fillers(c, v, first, last):
                            bank = BANK[task] if k is None else k % 2
                            freed(*held[bank])
                            if task == "Q":
                                queries(n + 1, (c + 1) % KC)
                                held[bank] = (task, n + 1)
                            elif task == "K":
                                keys((c + 1) % KC, b if c < KC - 1 else b + 1)
                                held[bank] = (task, n + 1)
                            elif task == "V":
                                values(k)
                                held[bank] = (task, b * QB + k)
                            elif task == "R":
                                turn_recips(n - 1)
                                held[bank] = (task, n - 1)
                            elif task == "WO":
                                project_out(b - 1, k)
                                held[bank] = (task, (b - 1) * QB + k)
                            else:
                                norm_turn((b + 1) * QB + k, k)
                                held[bank] = (task, (b + 1) * QB + k)

            def epilogue():
                u = NB * UNITS
                for v in range(LAG):
                    turn_probs(u - LAG + v, (v - LAG) % 4, UNITS - LAG + v)
                freed("R", NB - 2)
                turn_recips(NB - 1)
                freed("PV", NB - 2)
                values_of(NB - 1, KC - 1, B - 1)
                for i in range(QB):
                    freed(*(("PV", NB - 1), ("R", NB - 1), ("WO", (B - 1) * QB), ("WO", (B - 1) * QB + 1))[i])
                    project_out(B - 1, i)
                    if i == 1:
                        turn_block(0, 0, xb[0], "hn_ok", "hT_mm", "hT_hi")

            def turn_block(t, i, src, ok, done, hi):
                pe.wait_ge(s[ok], t + 1)
                if some(t):
                    pe.wait_ge(s[hi], t)
                if some(t):
                    pe.wait_ge(s[hi.replace("hi", "lo")], t)
                for k in range(KC):
                    mm = pe.transpose(h_ps[:, k * P:(k + 1) * P], src[:, k * P:(k + 1) * P], ident[:])
                mm.then_inc(s[done], 1)

            over_batches(pe, body, epilogue)

            pe.wait_ge(s["sel_ok"], BIAS_PARTS)
            pe.wait_ge(s["bias_put"], 16 * BIAS_PARTS)

            def route(t, i, more, loading):
                pe.wait_ge(s["hT_hi"], t + 1)
                pe.wait_ge(s["hT_lo"], t + 1)
                for e in range(NE):
                    if loading:
                        pe.wait_ge(s["fw_hi"], e + 1)
                        pe.wait_ge(s["fw_lo"], e + 1)
                    if some(t * NE + e - 3):
                        pe.wait_ge(s["lg_ok"], t * NE + e - 3)
                    bank = l_ps[e % 4]
                    pe.matmul(bank, bias_sel[:, e, :], bias_rows[:], start=True, stop=False)
                    for k in range(KC):
                        mm = three(pe, bank, hT_h[i][:, k, :], hT_l[i][:, k, :], w_h[:, e, k, :], w_l[:, e, k, :],
                                   False, k == KC - 1)
                    mm.then_inc(s["lg_mm"], 1)
                    if e == 3 and more:
                        turn_block(t + 1, 1 - i, xb[1 - i], "hn_ok", "hT_mm", "hT_hi")

            route(0, 0, True, True)
            route(1, 1, True, False)
            with pe.Fori(1, NT // 2 - 1) as pair:
                t = pair * 2
                for i in range(2):
                    route(t + i, i, True, False)
            route(NT - 2, 0, True, False)
            route(NT - 1, 1, False, False)

            def turn_c(t, i):
                pe.wait_ge(s["c_put"], t + 1)
                if some(t):
                    pe.wait_ge(s["cT_ok"], t)
                pe.transpose(c_ps[:, 0:P], c_pad[i][:], ident[:]).then_inc(s["cT_mm"], 1)

            def weigh_biases(t, i):
                pe.wait_ge(s["cT_ok"], t + 1)
                if some((t - 1) * (NE + 1) + 1):
                    pe.wait_ge(s["acc"], (t - 1) * (NE + 1) + 1)
                pe.matmul(b_ps[:], cT[i][:], eb[:], start=True, stop=True).then_inc(s["cb_mm"], 1)

            def experts(t, i, more, loading):
                pe.wait_ge(s["eT_hi"], t + 1)
                pe.wait_ge(s["eT_lo"], t + 1)
                if not loading:
                    weigh_biases(t, i)
                for e in range(NE):
                    if loading:
                        pe.wait_ge(s["ew_hi"], e + 1)
                        if e < POOL_LO:
                            pe.wait_ge(s["ew_lo_pool"], e + 1)
                        else:
                            pe.wait_ge(s["ew_lo"], e + 1 - POOL_LO)
                    if e >= 4:
                        pe.wait_ge(s["acc"], t * (NE + 1) + e - 2)
                    else:
                        if some(t * (NE + 1) + e - 3):
                            pe.wait_ge(s["acc"], t * (NE + 1) + e - 3)
                    for k in range(KC):
                        mm = three(pe, l_ps[e % 4], hT_h[i][:, k, :], hT_l[i][:, k, :], w_h[:, e, k, :],
                                   w_l[:, e, k, :], k == 0, k == KC - 1)
                    mm.then_inc(s["y_mm"], 1)
                    if e == 3 and loading:
                        pe.wait_ge(s["first_step"], (NT - 1) * FIRSTS)
                        turn_c(t, i)
                        pe.wait_ge(s["eb_hi"], 1)
                        pe.wait_ge(s["eb_lo"], 1)
                        weigh_biases(t, i)
                    if e == 3 and more:
                        turn_block(t + 1, 1 - i, hn, "en_ok", "eT_mm", "eT_hi")
                        turn_c(t + 1, 1 - i)

            pe.wait_ge(s["lg_ok"], NT * NE)
            turn_block(0, 0, hn, "en_ok", "eT_mm", "eT_hi")
            experts(0, 0, True, True)
            experts(1, 1, True, False)
            with pe.Fori(1, NT // 2 - 1) as pair:
                t = pair * 2
                for i in range(2):
                    experts(t + i, i, True, False)
            experts(NT - 2, 0, True, False)
            experts(NT - 1, 1, False, False)

        @block.scalar
        def _(act):
            def hi_weight(dst, src, name):
                act.wait_ge(s[name], 16)
                act.activation(dst[:], src[:], ACT.Copy).then_inc(s["w_hi"], 1)

            def turned_tokens(g, i):
                act.wait_ge(s["xT_mm"], g + 1)
                act.activation(xnT_h[:, :, i * P:(i + 1) * P], j_ps[i % 2][:].rearrange("p (k q) -> p k q", k=KC), ACT.Copy)\
                    .then_inc(s["xT_hi"], 1)

            def hi_of(n, part, name):
                act.wait_ge(s[name + "_mm"], n + 1)
                if some(n * (16 * STACK_DMAS)):
                    act.wait_ge(s["stacked"], n * (16 * STACK_DMAS))
                act.activation(qk[:, part], j_ps[BANK[name.upper()]][:], ACT.Copy, scale=SCALE if name == "q" else 1.0)\
                    .then_inc(s[name + "_hi"], 1)

            def copy_probs(u, n, v):
                i, hh = v // 2, 2 * (v % 2)
                act.wait_ge(s["turned"], u * 2 + 1)
                if some(n):
                    act.wait_ge(s["pv"], n)
                act.activation(pT[:, hh, 0:i + 1, i * P:(i + 1) * P],
                               t_ps[0][:, 0:(i + 1) * P].rearrange("p (k q) -> p k q", q=P), ACT.Copy)\
                    .then_inc(s["pt_act"], 1)

            hi_weight(wkv_h, wkv_raw, "wkv_in")
            turned_tokens(0, 0)
            hi_weight(wq_h, wq_raw, "wq_in")
            for i in range(1, QB):
                turned_tokens(i, i)
            hi_of(0, KH, "k")
            hi_of(0, QH, "q")
            hi_weight(wo_h, wo_raw, "wo_in")

            def body(b, first, last):
                for c in range(KC):
                    n = b * KC + c
                    for v in range(UNITS):
                        u = n * UNITS + v
                        i, slot, k = v // 2, v % 2, v % 4
                        w = (i + 1) * P
                        db, cc, vv = before(c, v)
                        if not (first and db < 0):
                            copy_probs(u - LAG, n if v >= LAG else n - 1, vv)
                        act.wait_ge(s["negmax"], u + 1)
                        if some((u - 3) * 2):
                            act.wait_ge(s["turned"], (u - 3) * 2)
                        if v == 0:
                            if some(n - 1):
                                act.wait_ge(s["recips"], n - 1)
                        for j in range(2):
                            hh = 2 * (v % 2) + j
                            e = act.activation(probs[:, k, j, 0:w], s_ps[slot][:, j, 0:w], ACT.Exp,
                                               bias=nmax[:, k, j:j + 1],
                                               accum_out=sums[:, c % 2, i, hh:hh + 1])
                        e.then_inc(s["exps"], 1)
                        for task, a in fillers(c, v, first, last):
                            if task == "Q":
                                hi_of(n + 1, QH, "q")
                            elif task == "K":
                                hi_of(n + 1, KH, "k")
                            elif task == "V":
                                act.wait_ge(s["v_mm"], b * QB + a + 1)
                                if some(b * KC):
                                    act.wait_ge(s["pv"], b * KC)
                                act.activation(v_sb[:, a, :], j_ps[a % 2][:], ACT.Copy).then_inc(s["v_ok"], 1)
                            elif task == "R":
                                act.wait_ge(s["r_mm"], n)
                                if some(n - 1):
                                    act.wait_ge(s["o_ok"], n - 1)
                                act.activation(r_sb[:], j_ps[BANK["R"]][:], ACT.Copy).then_inc(s["r_ok"], 1)
                            elif task == "LNT":
                                turned_tokens((b + 1) * QB + a, a)

            def epilogue():
                for v in range(LAG):
                    copy_probs(NB * UNITS - LAG + v, NB - 1, UNITS - LAG + v)
                act.wait_ge(s["r_mm"], NB)
                act.wait_ge(s["o_ok"], NB - 1)
                act.activation(r_sb[:], j_ps[BANK["R"]][:], ACT.Copy).then_inc(s["r_ok"], 1)
                act.wait_ge(s["pv"], NB)
                for e in range(NE):
                    act.wait_ge(s[f"raw{e}_in"], 16)
                    act.activation(w_h[:, e], w_raw[:, e], ACT.Copy).then_inc(s["fw_hi"], 1)
                    if e == 1:
                        hi_block(0, 0, "hT_mm", "lg_mm", "hT_hi")

            def hi_block(t, i, mm, used, hi):
                act.wait_ge(s[mm], t + 1)
                if some((t - 1) * NE):
                    act.wait_ge(s[used], (t - 1) * NE)
                act.activation(hT_h[i][:], h_ps[:].rearrange("p (k q) -> p k q", k=KC), ACT.Copy)\
                    .then_inc(s[hi], 1)

            over_batches(act, body, epilogue)

            def firsts(t, i, e, over=over, junk=junk[:]):
                at = t * FIRSTS + e * 3
                if e == 0:
                    if some(t - 1):
                        act.wait_ge(s["c_ok"], t - 1)
                for j in range(2):
                    if some(at - 2 * (1 - j)):
                        act.wait_ge(s["first_step"], at - 2 * (1 - j))
                    act.wait_ge(s["u_ok"], t * NE + e + j + 1)
                    act.activation(over[j], logits[i][:, e + j, :], ACT.Relu).then_inc(s["first_step"], 1)
                for j in range(2):
                    act.wait_ge(s["first_step"], at + 1 + j)
                    act.activation(junk, over[j], ACT.Sign, accum_out=sign_sum[:, i, e + j:e + j + 1])\
                        .then_inc(s["first_step"], 1)
                    act.wait_ge(s["first_step"], at + 3 + 2 * j)
                    act.activation(over[j], over[j], ACT.Tanh, scale=0.5,
                                   accum_out=tanh_sum[:, i, e + j:e + j + 1]).then_inc(s["first_step"], 1)

            def tanh_gap(t, i):
                act.wait_ge(s["gap_ok"], t + 1)
                if some(t):
                    act.wait_ge(s["w2_ok"], t)
                if some(t - 1):
                    act.wait_ge(s["c_ok"], t - 1)
                act.activation(th[:], gap[:], ACT.Tanh, scale=0.5, accum_out=th_sum[:, i:i + 1])\
                    .then_inc(s["th_ok"], 1)

            def hi_expert(e):
                act.wait_ge(s[f"raw{e}_in"], 32)
                act.activation(w_h[:, e], w_raw[:, e], ACT.Copy).then_inc(s["ew_hi"], 1)

            def route(t, i, more, behind=2):
                for e in range(NE):
                    if some(t - 1):
                        act.wait_ge(s["count"], (t - 2) * COUNTS + min(e + 2, COUNTS))
                        act.wait_ge(s["first_step"], (t - 2) * FIRSTS + (FIRSTS * 3 // 4 if e < 6 else FIRSTS))
                    act.wait_ge(s["lg_mm"], t * NE + e + 1)
                    act.activation(logits[i][:, e, :], l_ps[e % 4], ACT.Copy).then_inc(s["lg_ok"], 1)
                    if e == 0 and behind >= 2:
                        firsts(t - 2, i, 6)
                    if e == 3 and more:
                        hi_block(t + 1, 1 - i, "hT_mm", "lg_mm", "hT_hi")
                    if not more:
                        for k in {2: (0,), 3: (1, 2), 6: (3,), 7: (4,)}.get(e, ()):
                            hi_expert(k)
                    if e == 3 and behind:
                        tanh_gap(t - 1, 1 - i)
                    if e in (4, 5) and behind or e == 7 and more and behind:
                        firsts(t - 1, 1 - i, (4, 5, 7).index(e) * 2)

            route(0, 0, True, 0)
            route(1, 1, True, 1)
            with act.Fori(1, NT // 2 - 1) as pair:
                t = pair * 2
                for i in range(2):
                    route(t + i, i, True)
            route(NT - 2, 0, True)
            route(NT - 1, 1, False)

            hi_block(0, 0, "eT_mm", "y_mm", "eT_hi")
            firsts(NT - 2, 0, 4)
            hi_expert(5)
            act.wait_ge(s["eb_in"], 48)
            act.activation(eb[:], eb_raw[:], ACT.Copy).then_inc(s["eb_hi"], 1)
            firsts(NT - 2, 0, 6)
            hi_expert(6)
            hi_expert(7)
            act.wait_ge(s["cT_mm"], 1)
            act.activation(cT[0][:], c_ps[:, 0:P], ACT.Copy).then_inc(s["cT_ok"], 1)

            def experts(t, i):
                hi_block(t + 1, 1 - i, "eT_mm", "y_mm", "eT_hi")
                act.wait_ge(s["cT_mm"], t + 2)
                if some(t):
                    act.wait_ge(s["cb_mm"], t)
                act.activation(cT[1 - i][:], c_ps[:, 0:P], ACT.Copy).then_inc(s["cT_ok"], 1)

            spare = [top_b[:, 0], top_b[:, 1]]
            experts(0, 0)
            experts(1, 1)
            tanh_gap(NT - 1, 1)
            firsts(NT - 1, 1, 0, spare, top_b[:, 3])
            firsts(NT - 1, 1, 2, spare, top_b[:, 3])
            experts(2, 0)
            firsts(NT - 1, 1, 4, spare, top_b[:, 3])
            firsts(NT - 1, 1, 6, spare, top_b[:, 3])
            experts(3, 1)
            with act.Fori(2, NT // 2 - 1) as pair:
                t = pair * 2
                for i in range(2):
                    experts(t + i, i)
            experts(NT - 2, 0)

        @block.vector
        def _(dve):
            def statistics(g, slot, src, name):
                dve.bn_stats(stats[:, slot, :], src).then_inc(s[name + "_st"], 1)

            def mean_variance(g, slot, name):
                dve.wait_ge(s[name + "_st"], g + 1)
                if some((g + 1 - SLOTS[name]) * 2):
                    dve.wait_ge(s[name + "_rs"], (g + 1 - SLOTS[name]) * 2)
                dve.memset(turn[:], 0.0)
                dve.bn_aggr(moments[:, slot, :], stats[:, slot, :]).then_inc(s[name + "_var"], 1)

            def normed(g, slot, src, dst, name, ok):
                dve.wait_ge(s[name + "_rs"], (g + 1) * 2)
                dve.tensor_scalar(dst, src, moments[:, slot, 0:1], rstd[:, slot:slot + 1], ALU.subtract, ALU.mult)\
                    .then_inc(s[ok], 1)

            def lo_weight(k, dst, src, hi):
                dve.wait_ge(s["w_hi"], k + 1)
                dve.tensor_tensor(dst[:], src[:], f32(hi[:]), ALU.subtract).then_inc(s["w_lo"], 1)

            def block_statistics(b, i):
                if i == 0:
                    dve.wait_ge(s["x_in"], (b + 1) * 16)
                statistics(b * QB + i, i, xt[:, i, :], "ln")
                mean_variance(b * QB + i, i, "ln")

            def norm_block(b, i):
                if some(b * QB + i - 1):
                    dve.wait_ge(s["xT_mm"], b * QB + i - 1)
                normed(b * QB + i, i, xt[:, i, :], xn[:, i % 2, :], "ln", "xn_ok")

            def turned_tokens(g, i):
                dve.wait_ge(s["xT_hi"], g + 1)
                cols = slice(i * P, (i + 1) * P)
                dve.tensor_tensor(xnT_l[:, :, cols], j_ps[i % 2][:].rearrange("p (k q) -> p k q", k=KC),
                                  f32(xnT_h[:, :, cols]), ALU.subtract).then_inc(s["xT_lo"], 1)

            def lo_of(n, part, name):
                dve.wait_ge(s[name + "_hi"], n + 1)
                bank, hi = j_ps[BANK[name.upper()]], f32(qk[:, part - 1])
                if name == "q":
                    dve.scalar_tensor_tensor(qk[:, part], bank[:], SCALE, hi, ALU.mult, ALU.subtract)\
                        .then_inc(s["q_lo"], 1)
                else:
                    dve.tensor_tensor(qk[:, part], bank[:], hi, ALU.subtract).then_inc(s["k_lo"], 1)

            def copy_probs(u, n, v):
                i, hh = v // 2, 2 * (v % 2) + 1
                dve.wait_ge(s["turned"], u * 2 + 2)
                if some(n):
                    dve.wait_ge(s["pv"], n)
                dve.tensor_copy(pT[:, hh, 0:i + 1, i * P:(i + 1) * P],
                                t_ps[1][:, 0:(i + 1) * P].rearrange("p (k q) -> p k q", q=P)).then_inc(s["pt_dve"], 1)

            def reciprocals(n, c):
                dve.wait_ge(s["exps"], (n + 1) * UNITS)
                dve.reciprocal(recip[:], sums[:, c % 2]).then_inc(s["recips"], 1)
                dve.wait_ge(s["recips"], n + 1)
                if some(n):
                    dve.wait_ge(s["r_mm"], n)
                dve.tensor_copy(r_rep[:], recip[:].unsqueeze(3).broadcast_to([P, QB, HC, HD])).then_inc(s["reps"], 1)

            def scaled(n):
                dve.wait_ge(s["pv"], n + 1)
                dve.wait_ge(s["r_ok"], n + 1)
                if some(n):
                    dve.wait_ge(s["o_lo"], n)
                dve.tensor_tensor(o_sb[:], o_ps[:], r_sb[:], ALU.mult).then_inc(s["o_ok"], 1)

            def residual(b, i):
                if i == 0:
                    dve.wait_ge(s["xr_in"], (b + 1) * 16)
                dve.wait_ge(s["wo_mm"], b * QB + i + 1)
                dve.tensor_tensor(xr[:, i, :], j_ps[i % 2][:], xr[:, i, :], ALU.add).then_inc(s["x1_ok"], 1)

            for i in range(QB):
                block_statistics(0, i)
            norm_block(0, 0)
            norm_block(0, 1)
            lo_weight(0, wkv_l, wkv_raw, wkv_h)
            for i in range(2, QB):
                turned_tokens(i - 2, i - 2)
                norm_block(0, i)
            lo_weight(1, wq_l, wq_raw, wq_h)
            turned_tokens(2, 2)
            turned_tokens(3, 3)
            lo_of(0, KL, "k")
            lo_of(0, QL, "q")
            lo_weight(2, wo_l, wo_raw, wo_h)

            def body(b, first, last):
                for c in range(KC):
                    n = b * KC + c
                    for v in range(UNITS):
                        u = n * UNITS + v
                        i, slot, k = v // 2, v % 2, v % 4
                        w = (i + 1) * P
                        dve.wait_ge(s["scores"], u + 1)
                        if some(u - 3):
                            dve.wait_ge(s["exps"], u - 3)
                        dve.tensor_reduce(nmax[:, k, :], s_ps[slot][:, :, 0:w], AX_X, ALU.max, negate=True)\
                            .then_inc(s["negmax"], 1)
                        db, cc, vv = before(c, v)
                        if not (first and db < 0):
                            copy_probs(u - LAG, n if v >= LAG else n - 1, vv)
                        if v == 1 and not (first and c == 0):
                            reciprocals(n - 1, (c - 1) % KC)
                        cc, vv = (c, v - 1) if v else (c - 1, UNITS - 1)
                        for task, a in fillers(cc, vv, first, last) if cc >= 0 else ():
                            if task == "K":
                                lo_of(n + 1, KL, "k")
                            elif task == "WO":
                                residual(b - 1, a)
                            elif task == "LNT":
                                turned_tokens((b + 1) * QB + a, a)
                        if c == 1 and v in (1, 2, 4, 5) and not last:
                            block_statistics(b + 1, (1, 2, 4, 5).index(v))
                        if ("Q", None) in fillers(c, v, first, last):
                            lo_of(n + 1, QL, "q")
                        if v == 3 and not (first and c == 0):
                            scaled(n - 1)
                        if c == 2 and 2 <= v < 2 + QB and not last:
                            norm_block(b + 1, v - 2)

            def epilogue():
                for v in range(LAG):
                    copy_probs(NB * UNITS - LAG + v, NB - 1, UNITS - LAG + v)
                reciprocals(NB - 1, KC - 1)
                scaled(NB - 1)
                dve.memset(bias_rows[:], 0.0).then_inc(s["bias_zero"], 1)
                stats2(0, 0)
                mean_variance(0, 0, "ln2")
                norm2(0, 0)
                residual(B - 1, 0)
                split_bias()
                residual(B - 1, 1)
                lo_block(0, 0, "hT_hi", "hT_lo")
                lo_router(0)
                stats2(1, 1)
                mean_variance(1, 1, "ln2")
                residual(B - 1, 2)
                norm2(1, 1)
                lo_router(1)
                residual(B - 1, 3)
                for e in range(2, NE):
                    lo_router(e)

            def lo_block(t, i, hi, lo):
                dve.wait_ge(s[hi], t + 1)
                dve.tensor_tensor(hT_l[i][:], h_ps[:].rearrange("p (k q) -> p k q", k=KC), f32(hT_h[i][:]),
                                  ALU.subtract).then_inc(s[lo], 1)

            def stats2(t, i):
                dve.wait_ge(s["xb_in"], (t + 1) * 16)
                statistics(t, i, xb[i][:], "ln2")

            def norm2(t, i):
                normed(t, i, xb[i][:], xb[i][:], "ln2", "hn_ok")

            def lo_router(e):
                dve.wait_ge(s["fw_hi"], e + 1)
                dve.tensor_tensor(w_l[:, e], w_raw[:, e], f32(w_h[:, e]), ALU.subtract).then_inc(s["fw_lo"], 1)

            def split_bias():
                dve.wait_ge(s["bias_in"], 16)
                rows = slice(0, NE)
                dve.tensor_copy(bias_parts[rows, 0, :], bias_raw[rows, :]).then_inc(s["bias_split"], 1)
                dve.wait_ge(s["bias_split"], 1)
                dve.tensor_tensor(bias_rest[rows, :], bias_raw[rows, :], bias_parts[rows, 0, :], ALU.subtract)\
                    .then_inc(s["bias_rest_ok"], 1)
                dve.wait_ge(s["bias_rest_ok"], 1)
                dve.tensor_copy(bias_parts[rows, 1, :], bias_rest[rows, :]).then_inc(s["bias_split"], 1)
                dve.wait_ge(s["bias_split"], 2)
                dve.tensor_tensor(bias_parts[rows, 2, :], bias_rest[rows, :], bias_parts[rows, 1, :], ALU.subtract)\
                    .then_inc(s["bias_split"], 1)

            over_batches(dve, body, epilogue)


            dve.wait_ge(s["x1_out"], B * 16)

            STEPS = 7

            def top_two(t, i, ahead=False, between=lambda k: None):
                lg = logits[i]
                at = t * STEPS
                dve.wait_ge(s["lg_ok"], (t + 1) * NE)
                dve.tensor_tensor(top_a[:], lg[:, 0:4], lg[:, 4:8], ALU.max)
                if ahead:
                    mean_variance(t + 2, i, "ln2")
                between(0)
                dve.tensor_tensor(top_b[:], lg[:, 0:4], lg[:, 4:8], ALU.min).then_inc(s["top"], 1)
                if ahead:
                    norm2(t + 2, i)
                between(1)
                dve.wait_ge(s["top"], at + 1)
                if some(t * COUNTS):
                    dve.wait_ge(s["c_sum"], t * COUNTS)
                dve.tensor_tensor(top_c[:], top_a[:, 0:2], top_a[:, 2:4], ALU.max)
                between(2)
                dve.tensor_tensor(top_b[:, 0:2], top_b[:, 0:2], top_b[:, 2:4], ALU.max).then_inc(s["top"], 1)
                between(3)
                dve.tensor_tensor(top_a[:, 0:2], top_a[:, 0:2], top_a[:, 2:4], ALU.min).then_inc(s["top"], 1)
                dve.wait_ge(s["top"], at + 3)
                dve.tensor_tensor(top_b[:, 0:2], top_b[:, 0:2], top_a[:, 0:2], ALU.max).then_inc(s["top"], 1)
                between(4)
                dve.tensor_tensor(top_a[:, 3], top_c[:, 0], top_c[:, 1], ALU.min).then_inc(s["top"], 1)
                dve.tensor_tensor(top_a[:, 2], top_c[:, 0], top_c[:, 1], ALU.max).then_inc(s["top"], 1)
                dve.wait_ge(s["top"], at + 4)
                dve.tensor_tensor(top_b[:, 2], top_b[:, 0], top_b[:, 1], ALU.max).then_inc(s["top"], 1)
                between(5)
                dve.wait_ge(s["top"], at + 7)
                if some(t):
                    dve.wait_ge(s["u_ok"], t * NE)
                dve.tensor_tensor(second[:], top_a[:, 3], top_b[:, 2], ALU.max).then_inc(s["second_ok"], 1)
                between(6)
                dve.wait_ge(s["second_ok"], t + 1)
                if some(t):
                    dve.wait_ge(s["th_ok"], t)
                dve.tensor_tensor(gap[:], top_a[:, 2], second[:], ALU.subtract).then_inc(s["gap_ok"], 1)
                between(7)
                dve.wait_ge(s["gap_ok"], t + 1)
                dve.scalar_tensor_tensor(taken[:, 0, :], gap[:], 0.0, minus_one[:].broadcast_to([P, O]), ALU.is_equal,
                                         ALU.mult, accum_out=c_taken[:, i, 0:1]).then_inc(s["count"], 1)

            def finish_c(t, i, step):
                if step == 0:
                    dve.tensor_scalar(c_taken[:, i, NE:NE + 1], th_sum[:, i:i + 1], -0.5, 0.5 * O, ALU.mult, ALU.add)\
                        .then_inc(s["c_half"], 1)
                    dve.wait_ge(s["first_step"], (t + 1) * FIRSTS)
                    dve.tensor_tensor(c_first[:], tanh_sum[:, i, :], sign_sum[:, i, :], ALU.add)\
                        .then_inc(s["c_half"], 1)
                elif step == 1:
                    dve.wait_ge(s["c_half"], t * 3 + 1)
                    dve.tensor_tensor(c_diff[:], c_taken[:, i, 1:NE + 1], c_taken[:, i, 0:NE], ALU.subtract)\
                        .then_inc(s["c_half"], 1)
                else:
                    dve.wait_ge(s["c_half"], (t + 1) * 3)
                    dve.scalar_tensor_tensor(c_all[:, bass.ds(t, 1), :].rearrange("p a e -> p (a e)"), c_first[:],
                                             0.5, c_diff[:], ALU.mult, ALU.add).then_inc(s["c_ok"], 1)

            def weigh(t, i, behind, between=None):
                lg = logits[i]
                at = t * COUNTS
                if behind:
                    finish_c(t - 1, 1 - i, 0)
                dve.wait_ge(s["th_ok"], t + 1)
                dve.tensor_scalar(w2[:], th[:], -0.5, 0.5, ALU.mult, ALU.add).then_inc(s["w2_ok"], 1)
                if behind:
                    finish_c(t - 1, 1 - i, 1)
                for e in range(NE):
                    if between is not None:
                        between(e)
                    if e < NE - 1:
                        dve.wait_ge(s["u_ok"], t * NE + e + 1)
                        dve.wait_ge(s["count"], at + e + 1)
                        dve.scalar_tensor_tensor(taken[:, (e + 1) % 3, :], lg[:, e, :], 0.0, taken[:, e % 3, :],
                                                 ALU.is_equal, ALU.add).then_inc(s["count"], 1)
                    else:
                        dve.wait_ge(s["count"], at + e + 1)
                    if e == 0:
                        if behind:
                            finish_c(t - 1, 1 - i, 2)
                        dve.tensor_scalar(c_taken[:, i, 0:1], c_taken[:, i, 0:1], 0.5, None, ALU.mult)\
                            .then_inc(s["c_sum"], 1)
                        dve.wait_ge(s["w2_ok"], t + 1)
                    else:
                        dve.scalar_tensor_tensor(scrap[:, e % 2, :], taken[:, e % 3, :], 1.0, w2[:], ALU.min,
                                                 ALU.mult, accum_out=c_taken[:, i, e:e + 1]).then_inc(s["c_sum"], 1)

            def route(t, i, ahead, behind=True, between=None):
                if ahead:
                    stats2(t + 2, i)
                top_two(t, i, ahead)
                if ahead:
                    lo_block(t + 2, i, "hT_hi", "hT_lo")
                weigh(t, i, behind, between)

            lo_block(1, 1, "hT_hi", "hT_lo")
            route(0, 0, True, False)
            route(1, 1, True)
            with dve.Fori(1, NT // 2 - 1) as pair:
                t = pair * 2
                for i in range(2):
                    route(t + i, i, True)
            def stats3(t, i):
                dve.wait_ge(s["xe_in"], (t + 1) * 16)
                statistics(t, i, xb[i][:], "ln3")

            def norm3(t, i):
                if some(t):
                    dve.wait_ge(s["eT_mm"], t)
                normed(t, i, xb[i][:], hn[:], "ln3", "en_ok")

            def put_c(t, i):
                if some(t - 1):
                    dve.wait_ge(s["cT_mm"], t - 1)
                c_t = c_all[:, bass.ds(t, 1), :].rearrange("p a e -> p (a e)")
                dve.tensor_copy(c_hi[:], c_t).then_inc(s["c_hi_ok"], 1)
                dve.tensor_copy(c_now[i][:], c_t)
                dve.wait_ge(s["c_hi_ok"], t + 1)
                for g in range(2):
                    dve.tensor_copy(c_pad[i][:, g * HD:g * HD + NE], f32(c_hi[:]))
                dve.tensor_tensor(c_pad[i][:, 2 * HD:2 * HD + NE], c_t, f32(c_hi[:]), ALU.subtract)\
                    .then_inc(s["c_put"], 1)

            def first_moments(e):
                if e == 1:
                    stats3(0, 0)
                if e == 2:
                    mean_variance(0, 0, "ln3")
                    stats3(1, 1)
                if e == 3:
                    mean_variance(1, 1, "ln3")

            route(NT - 2, 0, False, between=first_moments)
            dve.wait_ge(s["pad_z"], 3)
            norm3(0, 0)
            put_c(0, 0)
            lo_block(0, 0, "eT_hi", "eT_lo")
            for e in range(POOL_LO, NE):
                dve.wait_ge(s["ew_hi"], e + 1)
                dve.tensor_tensor(w_l[:, e], w_raw[:, e], f32(w_h[:, e]), ALU.subtract).then_inc(s["ew_lo"], 1)
            dve.wait_ge(s["eb_hi"], 1)
            rows = slice(HD, HD + NE)
            dve.tensor_tensor(eb[rows, :], eb_raw[rows, :], f32(eb[rows, :]), ALU.subtract).then_inc(s["eb_lo"], 1)

            def expert(t, i, e, more):
                if e == 0:
                    dve.wait_ge(s["cb_mm"], t + 1)
                    dve.tensor_tensor(xb[i][:], b_ps[:], xb[i][:], ALU.add).then_inc(s["acc"], 1)
                dve.wait_ge(s["y_mm"], t * NE + e + 1)
                dve.wait_ge(s["acc"], t * (NE + 1) + e + 1)
                dve.scalar_tensor_tensor(xb[i][:], l_ps[e % 4], c_now[i][:, e:e + 1], xb[i][:], ALU.mult,
                                         ALU.add).then_inc(s["acc"], 1)
                if more and e == 1 and not (isinstance(t, int) and t == 0):
                    stats3(t + 1, 1 - i)
                if more and e == 2:
                    if not (isinstance(t, int) and t == 0):
                        mean_variance(t + 1, 1 - i, "ln3")
                    norm3(t + 1, 1 - i)
                    put_c(t + 1, 1 - i)
                if more and e == 3:
                    lo_block(t + 1, 1 - i, "eT_hi", "eT_lo")

            def experts(t, i, more):
                for e in range(NE):
                    expert(t, i, e, more)

            experts(0, 0, True)
            top_two(NT - 1, 1, between=lambda e: expert(1, 1, e, True))
            weigh(NT - 1, 1, True, lambda e: expert(2, 0, e, True))
            experts(3, 1, True)
            dve.wait_ge(s["c_sum"], NT * COUNTS)
            for step in range(3):
                finish_c(NT - 1, 1, step)
            with dve.Fori(2, NT // 2 - 1) as pair:
                t = pair * 2
                for i in range(2):
                    experts(t + i, i, True)
            experts(NT - 2, 0, True)
            experts(NT - 1, 1, False)

        @block.gpsimd
        def _(pool):
            pool.memset(ident[:], 0.0).then_inc(s["const_z"], 1)
            pool.memset(identb[:], 0.0).then_inc(s["const_z"], 1)
            pool.memset(maskb[:], 0.0).then_inc(s["const_z"], 1)
            pool.memset(minus_half[:], -0.5).then_inc(s["const_z"], 1)
            pool.memset(minus_one[:], -1.0).then_inc(s["const_z"], 1)
            pool.memset(eps[:], EPS).then_inc(s["const_z"], 1)
            pool.memset(zero[:], 0.0).then_inc(s["const_z"], 1)
            pool.wait_ge(s["const_z"], 7)
            for m in (ident, identb):
                pool.affine_select(out=m[:], in_=m[:], compare_op=ALU.not_equal, fill=1.0, base=0,
                                   pattern=[[-1, P]], channel_multiplier=1).then_inc(s["const_one"], 1)
            pool.affine_select(out=maskb[:], in_=maskb[:], compare_op=ALU.is_ge, fill=MASKED, base=0,
                               pattern=[[-1, P]], channel_multiplier=1).then_inc(s["const_mask"], 1)

            def split_context(b):
                pool.wait_ge(s["ctx_in"], (b + 1) * 16)
                if some(b * KC):
                    pool.wait_ge(s["k_mm"], b * KC)
                pool.tensor_tensor(ctx_h[:], ctx_raw[:], zero[:].broadcast_to([P, S]), ALU.add).then_inc(s["ctx_split"], 1)
                pool.wait_ge(s["ctx_split"], b * 2 + 1)
                pool.tensor_tensor(ctx_l[:], ctx_raw[:], f32(ctx_h[:]), ALU.subtract).then_inc(s["ctx_split"], 1)

            def split_outputs(n, c, b):
                pool.wait_ge(s["o_ok"], n + 1)
                if c == 0:
                    if some(b * QB):
                        pool.wait_ge(s["wo_mm"], b * QB)
                pool.tensor_tensor(oT_h[:, c, :], o_sb[:], zero[:].broadcast_to([P, S]), ALU.add).then_inc(s["o_hi"], 1)
                pool.wait_ge(s["o_hi"], n + 1)
                pool.tensor_tensor(oT_l[:, c, :], o_sb[:], f32(oT_h[:, c, :]), ALU.subtract).then_inc(s["o_lo"], 1)

            def deviation(g, slot, name):
                pool.wait_ge(s[name + "_var"], g + 1)
                if some(g + 1 - SLOTS[name]):
                    pool.wait_ge(s[{"ln": "xn_ok", "ln2": "hn_ok", "ln3": "en_ok"}[name]], g + 1 - SLOTS[name])
                r = rstd[:, slot:slot + 1]
                pool.tensor_tensor(r, moments[:, slot, 1:2], eps[:], ALU.add).then_inc(s[name + "_rs"], 1)
                pool.wait_ge(s[name + "_rs"], g * 2 + 1)
                pool.tensor_tensor(r, r, minus_half[:], ALU.pow).then_inc(s[name + "_rs"], 1)

            split_context(0)
            for i in range(QB):
                deviation(i, i, "ln")

            def body(b, first, last):
                for c in range(KC):
                    n = b * KC + c
                    if not (first and c == 0):
                        split_outputs(n - 1, (c - 1) % KC, b if c else b - 1)
                    if c == 1 and not last:
                        for i in range(QB):
                            deviation((b + 1) * QB + i, i, "ln")
                    if c == 2 and not last:
                        split_context(b + 1)

            def epilogue():
                split_outputs(NB - 1, KC - 1, B - 1)

            over_batches(pool, body, epilogue)

            pool.memset(bias_sel[:], 0.0).then_inc(s["sel_z"], 1)
            pool.wait_ge(s["sel_z"], 1)
            for k in range(BIAS_PARTS):
                if some(k):
                    pool.wait_ge(s["sel_ok"], k)
                pool.affine_select(out=bias_sel[:], in_=bias_sel[:], compare_op=ALU.not_equal, fill=1.0,
                                   base=-k * NE, pattern=[[-1, NE], [0, P]], channel_multiplier=1)\
                    .then_inc(s["sel_ok"], 1)

            def less_second(t, i):
                pool.wait_ge(s["second_ok"], t + 1)
                for e in range(NE):
                    pool.tensor_tensor(logits[i][:, e, :], logits[i][:, e, :], second[:], ALU.subtract)\
                        .then_inc(s["u_ok"], 1)

            deviation(0, 0, "ln2")
            deviation(1, 1, "ln2")
            with pool.Fori(0, NT // 2 - 1) as pair:
                t = pair * 2
                for i in range(2):
                    deviation(t + i + 2, i, "ln2")
                    less_second(t + i, i)

            def lo_expert(e):
                pool.wait_ge(s["ew_hi"], e + 1)
                pool.tensor_tensor(w_l[:, e], w_raw[:, e], f32(w_h[:, e]), ALU.subtract)\
                    .then_inc(s["ew_lo_pool"], 1)

            lo_expert(0)
            less_second(NT - 2, 0)
            pool.wait_ge(s["u_ok"], (NT - 1) * NE)
            pool.wait_ge(s["count"], (NT - 2) * COUNTS + NE // 2 + 1)
            pool.wait_ge(s["first_step"], (NT - 2) * FIRSTS + FIRSTS // 2)
            for m in (eb_raw, c_pad[0], c_pad[1]):
                pool.memset(m[:], 0.0).then_inc(s["pad_z"], 1)
            deviation(0, 0, "ln3")
            for e in range(1, POOL_LO):
                lo_expert(e)
            deviation(1, 1, "ln3")
            deviation(2, 0, "ln3")
            less_second(NT - 1, 1)
            deviation(3, 1, "ln3")
            with pool.Fori(2, NT // 2) as pair:
                t = pair * 2
                for i in range(2):
                    deviation(t + i, i, "ln3")


_OUT = "out_0_dram"


def kernel(x, ctx_512, L0_xattn_Wq, L0_xattn_Wkv_expand, L0_xattn_Wout, L0_ffn_router_w, L0_ffn_router_b,
           L0_ffn_expert_w, L0_ffn_expert_b):
    import numpy as np
    import concourse.bacc as bacc
    from concourse.bass_utils import run_bass_kernel_spmd

    arrays = {
        "x": np.asarray(x).reshape(B * S, H),
        "ctxT": np.asarray(ctx_512)[:, :S, :].transpose(0, 2, 1).reshape(B * P, S),
        "wqT": np.asarray(L0_xattn_Wq).T,
        "wkvT": np.asarray(L0_xattn_Wkv_expand).T,
        "woT": np.asarray(L0_xattn_Wout).T,
        "routerT": np.asarray(L0_ffn_router_w).reshape(O, NE, H).transpose(2, 1, 0),
        "router_b": np.asarray(L0_ffn_router_b).reshape(O, NE).T,
        "expertT": np.asarray(L0_ffn_expert_w).transpose(2, 0, 1),
        "expert_b": np.asarray(L0_ffn_expert_b),
    }
    arrays = {f"in_{n}": np.ascontiguousarray(a) for n, a in arrays.items()}
    nc = bacc.Bacc("TRN2", target_bir_lowering=False, num_devices=1)
    args = [nc.dram_tensor(n, a.shape, mybir.dt.from_np(a.dtype), kind="ExternalInput").ap()
            for n, a in arrays.items()]
    out = nc.dram_tensor(_OUT, (B * S, H), F32, kind="ExternalOutput").ap()
    build(nc, *args, out)
    r = run_bass_kernel_spmd(nc, [arrays], core_ids=[0])
    return np.asarray(r.results[0][_OUT]).reshape(B, S, H)
```
